# Optimizing a Trainium2 kernel written in Bass

```python
import numpy as np
import jax
import jax.numpy as jnp

def _softmax(x, axis=-1):
    return jax.nn.softmax(x, axis=axis)

def _gelu(x):
    return jax.nn.gelu(x, approximate=True)

def _silu(x):
    return jax.nn.silu(x)

def _sigmoid(x):
    return jax.nn.sigmoid(x)

def _layernorm(x, axis=-1, eps=1e-05):
    m = jnp.mean(x, axis=axis, keepdims=True)
    v = jnp.var(x, axis=axis, keepdims=True)
    return (x - m) / jnp.sqrt(v + eps)

def _scatter_add(tgt, idx, src, axis=0):
    return tgt.at[idx].add(src)

def _segment_sum(src, seg, n):
    return jax.ops.segment_sum(src, seg, n)
kernel_name = 'mk_seq_preln_d1_jaxref_r4_28f100'

def setup_inputs(seed: int=0):
    np.random.seed(seed)
    _w = jnp.asarray

    def _L0_attn_setup():
        import jax, jax.numpy as jnp
        import numpy as np
        D = 512
        EPS = 1e-05

        def _hgrn_scan(a, b):

            def comb(c1, c2):
                a1, b1 = c1
                a2, b2 = c2
                return (a1 * a2, b1 * a2 + b2)
            _, h = jax.lax.associative_scan(comb, (a, b), axis=1)
            return h
        key = jax.random.key(seed)
        ks = jax.random.split(key, 6)
        B, T = (4, 1024)
        gain = 2 ** (-2.5)
        scale = gain * np.sqrt(6.0 / (D + D))

        def w(k):
            return jax.random.uniform(k, (D, D), jnp.float32, -scale, scale)
        return {'hidden_states': jax.random.normal(ks[0], (B, T, D), jnp.float32), 'Wi': w(ks[1]), 'Wf': w(ks[2]), 'Wg': w(ks[3]), 'Wo': w(ks[4]), 'g_norm_weight': jnp.ones((D,), jnp.float32)}
    _L0_attn_in = _L0_attn_setup()

    def _L0_ffn_setup():
        import jax, jax.numpy as jnp
        import numpy as np
        B_, S_, H_, O_ = (4, 512, 512, 512)
        E_, R_ = (8, 16)
        LORA_ALPHA = 16.0
        key = jax.random.key(seed)
        ks = jax.random.split(key, 5)
        x = jax.random.normal(ks[0], (B_, S_, H_), dtype=jnp.float32)
        W = jax.random.normal(ks[1], (O_, H_), dtype=jnp.float32) * 0.02
        gate_w = jax.random.normal(ks[2], (E_, H_), dtype=jnp.float32) * 0.02
        A = jax.random.normal(ks[3], (E_, R_, H_), dtype=jnp.float32) * 0.02
        B = jax.random.normal(ks[4], (E_, O_, R_), dtype=jnp.float32) * 0.02
        return {'x': x, 'W': W, 'gate_w': gate_w, 'A': A, 'B': B}
    _L0_ffn_in = _L0_ffn_setup()
    _d = {'L0_attn_hidden_states': _L0_attn_in['hidden_states'], 'L0_attn_Wi': _L0_attn_in['Wi'], 'L0_attn_Wf': _L0_attn_in['Wf'], 'L0_attn_Wg': _L0_attn_in['Wg'], 'L0_attn_Wo': _L0_attn_in['Wo'], 'L0_attn_g_norm_weight': _L0_attn_in['g_norm_weight'], 'L0_ffn_W': _L0_ffn_in['W'], 'L0_ffn_gate_w': _L0_ffn_in['gate_w'], 'L0_ffn_A': _L0_ffn_in['A'], 'L0_ffn_B': _L0_ffn_in['B']}
    _x0 = _d['L0_attn_hidden_states']
    _d['L0_attn_hidden_states'] = jax.random.normal(jax.random.fold_in(jax.random.key(seed), 1), (2, 2048, 512), dtype=_x0.dtype)
    del _x0
    return _d

def reference(L0_attn_hidden_states, L0_attn_Wi, L0_attn_Wf, L0_attn_Wg, L0_attn_Wo, L0_attn_g_norm_weight, L0_ffn_W, L0_ffn_gate_w, L0_ffn_A, L0_ffn_B):

    def _L0_attn_ref(hidden_states, Wi, Wf, Wg, Wo, g_norm_weight):
        import jax, jax.numpy as jnp
        import numpy as np
        D = 512
        EPS = 1e-05

        def _hgrn_scan(a, b):

            def comb(c1, c2):
                a1, b1 = c1
                a2, b2 = c2
                return (a1 * a2, b1 * a2 + b2)
            _, h = jax.lax.associative_scan(comb, (a, b), axis=1)
            return h
        x = hidden_states
        i_raw = jnp.einsum('btd,de->bte', x, Wi)
        f_raw = jnp.einsum('btd,de->bte', x, Wf)
        i = jax.nn.silu(i_raw) * jax.nn.sigmoid(-f_raw)
        a = jnp.exp(jax.nn.log_sigmoid(f_raw))
        o = _hgrn_scan(a, i)
        g = jnp.einsum('btd,de->bte', x, Wg)
        rms = o * jax.lax.rsqrt(jnp.mean(o * o, axis=-1, keepdims=True) + EPS)
        o = rms * g_norm_weight * (g * jax.nn.sigmoid(g))
        return jnp.einsum('btd,de->bte', o, Wo)

    def _L0_ffn_ref(x, W, gate_w, A, B):
        import jax, jax.numpy as jnp
        import numpy as np
        B_, S_, H_, O_ = (4, 512, 512, 512)
        E_, R_ = (8, 16)
        LORA_ALPHA = 16.0
        bsz, seq, hid = x.shape
        E = gate_w.shape[0]
        x_flat = x.reshape(-1, hid)
        out = x_flat @ W.T
        logits = x_flat @ gate_w.T
        probs = jax.nn.softmax(logits, axis=-1)
        topk_w, topk_idx = jax.lax.top_k(probs, 2)
        topk_w = topk_w / jnp.sum(topk_w, axis=-1, keepdims=True)
        onehot = jax.nn.one_hot(topk_idx, E, dtype=x.dtype)
        wmat = jnp.einsum('tk,tke->te', topk_w, onehot) * LORA_ALPHA
        h = jnp.einsum('th,erh->etr', x_flat, A)
        hw = h * wmat.T[:, :, None]
        lora = jnp.einsum('etr,eor->to', hw, B)
        return (out + lora).reshape(bsz, seq, -1)
    x = L0_attn_hidden_states
    x = x + _L0_attn_ref(_layernorm(x, axis=-1), L0_attn_Wi, L0_attn_Wf, L0_attn_Wg, L0_attn_Wo, L0_attn_g_norm_weight)
    x = x + _L0_ffn_ref(_layernorm(x, axis=-1), L0_ffn_W, L0_ffn_gate_w, L0_ffn_A, L0_ffn_B)
    return x

_drawn_inputs = setup_inputs


def setup_inputs(seed=0):
    import zlib

    import numpy as np

    out = dict(_drawn_inputs(seed))
    spreads = {'L0_attn_g_norm_weight': (1.0, 0.6)}
    factors = {'L0_attn_Wf': 4.79}
    for name, (base, spread) in spreads.items():
        noise = np.random.default_rng([zlib.crc32(name.encode()), seed]).standard_normal(out[name].shape)
        drawn = base * np.exp(spread * noise) if base else spread * noise
        out[name] = jnp.asarray(drawn.astype(out[name].dtype))
    for name, factor in factors.items():
        out[name] = (out[name] * factor).astype(out[name].dtype)
    return out
```

```python
from collections import namedtuple
from contextlib import ExitStack

import concourse.bass as bass
from concourse import mybir

Block = namedtuple("Block", "j par tb")


def hgrn_lora_moe(nc, x_in, gn_in, wproj_in, wo_in, wffn_in, wb_in, out):
    F32, F32R, U32 = mybir.dt.float32, mybir.dt.float32r, mybir.dt.uint32
    ALU, ACT = mybir.AluOpType, mybir.ActivationFunctionType

    P = 128
    NSEQ, SEQ, D = x_in.shape
    NT = 4
    TOK = NT * P
    NBLK = NSEQ * SEQ // TOK
    NK = D // P
    ER = wb_in.shape[0]
    FW = wffn_in.shape[2]
    E = FW - D - ER
    R = ER // E
    HALF = FW // 2
    REST = D - HALF
    EPS, ALPHA = 1e-5, 16.0
    PROJ = 3 * NK * P
    QF, QI, QG = range(3)

    x_v = x_in.rearrange("b (t n p) d -> b t p n d", n=NT, p=P)
    out_v = out.rearrange("b (t n p) d -> b t n p d", n=NT, p=P)

    ctx = ExitStack()
    with ctx:
        def sb(name, shape, dt=F32):
            return ctx.enter_context(nc.sbuf_tensor(name, shape, dt))

        def pb(name):
            return ctx.enter_context(nc.psum_tensor(name, [P, 512], F32))

        def sem(name):
            return ctx.enter_context(nc.semaphore(name))

        wproj_h = sb("wproj_h", [P, NK, 3, NK, P], F32R)
        wproj_l = sb("wproj_l", [P, NK, 3, NK, P], F32R)
        wo_h = sb("wo_h", [P, NK, D], F32R)
        wo_l = sb("wo_l", [P, NK, D], F32R)
        wffn_h = sb("wffn_h", [P, NK, FW], F32R)
        wffn_l = sb("wffn_l", [P, NK, FW], F32R)
        wb_h = sb("wb_h", [ER, D], F32R)
        wb_l = sb("wb_l", [ER, D], F32R)
        gn = sb("gn", [P, NK])
        x = [sb(f"x_seq{i}", [P, NT, D]) for i in range(2)]
        x1 = sb("x1", [P, NT, D])
        xn = sb("xn", [P, NT, D])
        outb = sb("outb", [P, 2, D])
        xnT_h = sb("xnT_h", [P, NK, TOK], F32R)
        xnT_l = sb("xnT_l", [P, NK, TOK], F32R)
        x2T_h = sb("x2T_h", [P, NK, TOK], F32R)
        x2T_l = sb("x2T_l", [P, NK, TOK], F32R)
        ogT_h = sb("ogT_h", [P, NK, TOK], F32R)
        ogT_l = sb("ogT_l", [P, NK, TOK], F32R)
        decay = sb("decay", [P, TOK])
        inject = sb("inject", [P, TOK])
        value = sb("value", [P, TOK])
        gate = sb("gate", [P, TOK])
        o = sb("o", [P, TOK])
        og = sb("og", [P, TOK])
        osq = sb("osq", [P, TOK])
        osum = sb("osum", [P, TOK])
        carry = sb("carry", [P, NSEQ, NK])
        h = sb("h", [P, NT, ER + E])
        top = sb("top", [P, NT, 8])
        topi = sb("topi", [P, NT, 8], U32)
        gap = sb("gap", [P, NT])
        topw = sb("topw", [P, NT, 2])
        pick = sb("pick", [P, NT, 2, E])
        wmat = sb("wmat", [P, NT, E])
        hw = sb("hw", [P, NT, ER])
        hwT_h = sb("hwT_h", [ER, TOK], F32R)
        hwT_l = sb("hwT_l", [ER, TOK], F32R)
        bn1, mv1, ve1, rstd1 = (sb(n, s) for n, s in (("bn1", [P, NT, 6]), ("mv1", [P, NT, 2]), ("ve1", [P, NT]), ("rstd1", [P, NT])))
        bn2, mv2, ve2, rstd2 = (sb(n, s) for n, s in (("bn2", [P, NT, 6]), ("mv2", [P, NT, 2]), ("ve2", [P, NT]), ("rstd2", [P, NT])))
        ms, rr = sb("ms", [P, NT]), sb("rr", [P, NT])
        ident = sb("ident", [P, P])
        ones = sb("ones", [P, 1])
        minus_half = sb("minus_half", [P, NT])
        expert_no = sb("expert_no", [P, E])

        bank = [pb(n) for n in ("psum_f", "psum_i", "psum_g")]
        tp = [pb("psum_t0"), pb("psum_t1")]
        main = [pb(f"psum_m{i}") for i in range(3)]

        def main_e1(n):
            return main[n % 3]

        def main_e2(n):
            return main[(NT + n) % 3]

        def main_c(n):
            return main[(2 * NT + n) % 3]

        s_x = [sem("x0_loaded"), sem("x1_loaded")]
        s_stage = [sem(f"stage{i}_loaded") for i in range(4)]
        s_gn = sem("gn_loaded")
        s_out = [sem("out0_stored"), sem("out1_stored")]
        s_const = sem("constants_made")
        s_ident = sem("ident_zeroed")
        s_gnw = sem("wo_scaled")
        s_whi, s_wlo = sem("weights_hi"), sem("weights_lo")
        s_proj = [sem("f_done"), sem("i_done"), sem("g_done")]
        s_t1, s_t2, s_hwt = sem("t1_done"), sem("t2_done"), sem("hwt_done")
        s_e1, s_e2, s_rms, s_c = sem("e1_done"), sem("e2_done"), sem("rms_done"), sem("c_done")
        s_decay, s_inject, s_value, s_gate = sem("decay_ready"), sem("inject_ready"), sem("value_ready"), sem("gate_ready")
        s_sq, s_oghi = sem("osq_ready"), sem("og_hi")
        s_t1hi, s_t2hi, s_hwhi = sem("t1_hi"), sem("t2_hi"), sem("hw_hi")
        s_h, s_topw = sem("h_copied"), sem("topw_ready")
        s_u, s_v, s_scan, s_carry = sem("silu_i"), sem("scan_input"), sem("scan_done"), sem("carry_saved")
        s_w, s_og, s_oglo, s_osum = sem("silu_g"), sem("og_ready"), sem("og_lo"), sem("osum_ready")
        s_t1lo, s_t2lo, s_hwlo = sem("t1_lo"), sem("t2_lo"), sem("hw_lo")
        s_x1w, s_top, s_topi, s_gap = sem("x1_rest"), sem("top_ready"), sem("topi_ready"), sem("gap_ready")
        s_eq, s_pick, s_wmat, s_hw = sem("eq_ready"), sem("pick_ready"), sem("wmat_ready"), sem("hw_ready")
        s_ob, s_ms, s_x1 = sem("out_ready"), sem("ms_ready"), sem("x1_ready")
        s_bn1, s_mv1, s_ve1, s_xn1 = sem("bn1_done"), sem("mv1_done"), sem("ve1_ready"), sem("xn1_ready")
        s_bn2, s_mv2, s_ve2, s_xn2 = sem("bn2_done"), sem("mv2_done"), sem("ve2_ready"), sem("xn2_ready")
        s_zero = sem("carry_zeroed")
        s_rstd1, s_rr, s_rstd2 = sem("rstd1_ready"), sem("rr_ready"), sem("rstd2_ready")

        def flow(eng, step):
            step(None, Block(0, 0, 0), Block(1, 1, 0))
            with eng.Fori(0, (NBLK - 2) // 2) as k:
                step(Block(2 * k, 0, k), Block(2 * k + 1, 1, k), Block(2 * k + 2, 0, k + 1))
                step(Block(2 * k + 1, 1, k), Block(2 * k + 2, 0, k + 1), Block(2 * k + 3, 1, k + 1))
            step(Block(NBLK - 2, 0, NBLK // 2 - 1), Block(NBLK - 1, 1, NBLK // 2 - 1), None)

        def first(b, j):
            return isinstance(b.j, int) and b.j == j

        LAST = Block(NBLK - 1, 1, NBLK // 2 - 1)

        AREAS = [x1, x[1], xn, outb]
        GROUPS = []

        def group(area, width, src, hi, lo):
            stage = AREAS[area][:, :, :].rearrange("p n d -> p (n d)")[:, 0:width]
            before = sum(g[4] == area for g in GROUPS)
            GROUPS.append((src, stage, hi, lo, area, before))

        def flat(ap):
            return ap.rearrange("p k n -> p (k n)")

        for c, area in enumerate((0, 1, 2, 0)):
            group(area, PROJ, wproj_in[c], wproj_h[:, c].rearrange("p q k n -> p (q k n)"),
                  wproj_l[:, c].rearrange("p q k n -> p (q k n)"))
        G_WO = len(GROUPS)
        group(2, NK * D, flat(wo_in), flat(wo_h[:, :, :]), flat(wo_l[:, :, :]))
        for area, ks in ((0, slice(0, NK // 2)), (2, slice(NK // 2, NK))):
            group(area, NK // 2 * FW, flat(wffn_in[:, ks, :]), flat(wffn_h[:, ks, :]), flat(wffn_l[:, ks, :]))
        group(3, D, wb_in, wb_h[:, :], wb_l[:, :])
        AHEAD = [[1], [2, 3], [G_WO], [G_WO + 1, G_WO + 2, G_WO + 3]]

        block = ctx.enter_context(nc.Block())

        @block.sync
        def _(sp):
            def load_x(b):
                sp.dma_start(x[b.par][:, :, :], x_v[b.par, b.tb]).then_inc(s_x[b.par], 16)

            def store_out(b):
                for n in range(NT):
                    sp.wait_ge(s_ob, NT * b.j + n + 1)
                    sp.dma_start(out_v[b.par, b.tb, n], outb[:, n % 2, :]).then_inc(s_out[n % 2], 16)

            def load_group(g):
                src, stage, _, _, area, before = GROUPS[g]
                if before:
                    sp.wait_ge(s_wlo, 1 + max(i for i in range(g) if GROUPS[i][4] == area))
                elif area == 2:
                    sp.wait_ge(s_t1, NK)
                sp.dma_start(stage, src).then_inc(s_stage[area], 16)

            load_x(Block(0, 0, 0))
            load_group(0)
            load_group(1)
            sp.dma_start(gn[:, :], gn_in).then_inc(s_gn, 16)
            load_group(2)
            load_group(3)
            sp.wait_ge(s_wlo, 2)
            load_x(Block(1, 1, 0))
            for g in range(G_WO, len(GROUPS)):
                load_group(g)

            def step(prev, now, nxt):
                if prev is not None:
                    if nxt is not None:
                        sp.wait_ge(s_x1, NT * now.j)
                        load_x(nxt)
                    store_out(prev)

            flow(sp, step)
            store_out(LAST)
            for i in range(2):
                sp.wait_ge(s_out[i], NBLK * NT // 2 * 16)

        @block.gpsimd
        def _(pool):
            nc.gpsimd.memset(ident[:, :], 0.0).then_inc(s_ident, 1)
            pool.wait_ge(s_ident, 1)
            nc.gpsimd.affine_select(out=ident[:, :], in_=ident[:, :], compare_op=ALU.not_equal, fill=1.0,
                                    base=0, pattern=[[-1, P]], channel_multiplier=1).then_inc(s_const, 1)
            nc.gpsimd.memset(ones[:, :], 1.0).then_inc(s_const, 1)
            nc.gpsimd.memset(minus_half[:, :], -0.5).then_inc(s_const, 1)
            for e in range(E):
                nc.gpsimd.memset(expert_no[:, e:e + 1], float(e)).then_inc(s_const, 1)
            pool.wait_ge(s_const, 3)

            def norm1(b):
                pool.wait_ge(s_ve1, 2 * b.j + 2)
                nc.gpsimd.tensor_tensor(rstd1[:, :], ve1[:, :], minus_half[:, :], ALU.pow).then_inc(s_rstd1, 1)

            norm1(Block(0, 0, 0))

            def step(prev, now, nxt):
                if nxt is not None:
                    norm1(nxt)
                pool.wait_ge(s_ms, now.j + 1)
                nc.gpsimd.tensor_tensor(rr[:, :], ms[:, :], minus_half[:, :], ALU.pow).then_inc(s_rr, 1)
                for n in range(NT):
                    pool.wait_ge(s_ve2, NT * now.j + n + 1)
                    nc.gpsimd.tensor_tensor(rstd2[:, n:n + 1], ve2[:, n:n + 1], minus_half[:, 0:1],
                                            ALU.pow).then_inc(s_rstd2, 1)

            flow(pool, step)

        @block.scalar
        def _(act):
            def split_weights(g):
                _, stage, hi, _, area, before = GROUPS[g]
                if g == G_WO:
                    act.wait_ge(s_gnw, NK)
                else:
                    act.wait_ge(s_stage[area], 16 * (before + 1))
                nc.scalar.activation(hi, stage, ACT.Copy).then_inc(s_whi, 1)

            def t1_hi(b, k):
                act.wait_ge(s_t1, NK * b.j + k + 1)
                nc.scalar.activation(xnT_h[:, k, :], tp[(k + 1) % 2][:, :], ACT.Copy).then_inc(s_t1hi, 1)

            def t2_hi(b, k):
                act.wait_ge(s_t2, NK * b.j + k + 1)
                nc.scalar.activation(x2T_h[:, k, :], tp[k % 2][:, :], ACT.Copy).then_inc(s_t2hi, 1)

            def forget(b, c):
                act.wait_ge(s_proj[QF], NK * b.j + c + 1)
                if not (first(b, 0) and c == 0):
                    act.wait_ge(s_scan, NK * b.j + c)
                nc.scalar.activation(decay[:, :], bank[QF][:, :], ACT.Sigmoid).then_inc(s_decay, 1)
                nc.scalar.activation(inject[:, :], bank[QF][:, :], ACT.Sigmoid, scale=-1.0).then_inc(s_inject, 1)

            def put(b, c):
                act.wait_ge(s_proj[QI], NK * b.j + c + 1)
                nc.scalar.activation(value[:, :], bank[QI][:, :], ACT.Sigmoid).then_inc(s_value, 1)

            def output_gate(b, c):
                act.wait_ge(s_proj[QG], NK * b.j + c + 1)
                if not (first(b, 0) and c == 0):
                    act.wait_ge(s_og, NK * b.j + c)
                nc.scalar.activation(gate[:, :], bank[QG][:, :], ACT.Sigmoid).then_inc(s_gate, 1)

            def square(b, c):
                act.wait_ge(s_scan, NK * b.j + c + 1)
                if c == 0:
                    if not first(b, 0):
                        act.wait_ge(s_rms, b.j)
                    dst = osum
                else:
                    if c == 1 and not first(b, 0):
                        act.wait_ge(s_osum, (NK - 1) * b.j)
                    elif c > 1:
                        act.wait_ge(s_osum, (NK - 1) * b.j + c - 1)
                    dst = osq
                nc.scalar.activation(dst[:, :], o[:, :], ACT.Square).then_inc(s_sq, 1)

            def og_hi(b, c):
                act.wait_ge(s_og, NK * b.j + c + 1)
                if c == 0 and not first(b, 0):
                    act.wait_ge(s_c, NT * b.j)
                nc.scalar.activation(ogT_h[:, c, :], og[:, :], ACT.Copy).then_inc(s_oghi, 1)

            def expert_inputs(b):
                for n in range(NT):
                    act.wait_ge(s_e1, NT * b.j + n + 1)
                    nc.scalar.activation(h[:, n, :], main_e1(n)[:, REST:HALF], ACT.Copy).then_inc(s_h, 1)
                act.wait_ge(s_gap, b.j + 1)
                nc.scalar.activation(topw[:, :, 0], gap[:, :], ACT.Sigmoid).then_inc(s_topw, 1)
                nc.scalar.activation(topw[:, :, 1], gap[:, :], ACT.Sigmoid, scale=-1.0).then_inc(s_topw, 1)

            def hw_hi(b):
                act.wait_ge(s_hwt, b.j + 1)
                nc.scalar.activation(hwT_h[:, :], tp[0][:, :], ACT.Copy).then_inc(s_hwhi, 1)

            split_weights(0)
            for k in range(NK):
                t1_hi(Block(0, 0, 0), k)

            def step(prev, now, nxt):
                for c in range(NK):
                    if prev is None:
                        for g in AHEAD[c]:
                            split_weights(g)
                    forget(now, c)
                    if prev is not None and c == 1:
                        t2_hi(prev, 2)
                    put(now, c)
                    if prev is not None and c == 1:
                        t2_hi(prev, 3)
                    if prev is not None and c == 3:
                        hw_hi(prev)
                    output_gate(now, c)
                    square(now, c)
                    if prev is not None and c == 0:
                        t2_hi(prev, 0)
                        t2_hi(prev, 1)
                    og_hi(now, c)
                    if prev is not None and c == 1:
                        expert_inputs(prev)
                if nxt is not None:
                    for k in range(NK):
                        t1_hi(nxt, k)
                if prev is not None:
                    act.wait_ge(s_hw, prev.j + 1)

            flow(act, step)
            for k in range(NK):
                t2_hi(LAST, k)
            expert_inputs(LAST)
            hw_hi(LAST)

        @block.vector
        def _(dve):
            def split_weights(g):
                _, stage, hi, lo, area, before = GROUPS[g]
                if g == G_WO:
                    dve.wait_ge(s_stage[area], 16 * (before + 1))
                    dve.wait_ge(s_gn, 16)
                    for k in range(NK):
                        part = stage[:, k * D:(k + 1) * D]
                        nc.vector.tensor_scalar(part, part, gn[:, k:k + 1], None, ALU.mult).then_inc(s_gnw, 1)
                dve.wait_ge(s_whi, g + 1)
                nc.vector.tensor_tensor(lo, stage, hi.bitcast(F32), ALU.subtract).then_inc(s_wlo, 1)

            def norm1_stats(b):
                dve.wait_ge(s_x[b.par], 16 * (b.tb + 1))
                for n in range(NT):
                    if n > 0:
                        dve.wait_ge(s_bn1, NT * b.j + n)
                    nc.vector.bn_stats(bn1[:, n, :], x[b.par][:, n, :]).then_inc(s_bn1, 1)
                    if n > 0:
                        nc.vector.bn_aggr(mv1[:, n - 1, :], bn1[:, n - 1, :]).then_inc(s_mv1, 1)
                dve.wait_ge(s_mv1, NT * b.j + NT - 1)
                dve.wait_ge(s_bn1, NT * b.j + NT)
                nc.vector.tensor_scalar(ve1[:, 0:NT - 1], mv1[:, 0:NT - 1, 1], EPS, None, ALU.add).then_inc(s_ve1, 1)
                nc.vector.bn_aggr(mv1[:, NT - 1, :], bn1[:, NT - 1, :]).then_inc(s_mv1, 1)
                dve.wait_ge(s_mv1, NT * b.j + NT)
                nc.vector.tensor_scalar(ve1[:, NT - 1:NT], mv1[:, NT - 1, 1:2], EPS, None, ALU.add).then_inc(s_ve1, 1)

            def norm1_apply(b):
                dve.wait_ge(s_rstd1, b.j + 1)
                if not first(b, 0) and not first(b, 1):
                    dve.wait_ge(s_t2, NK * (b.j - 1))
                for n in range(NT):
                    nc.vector.tensor_scalar(xn[:, n, :], x[b.par][:, n, :], mv1[:, n, 0:1], rstd1[:, n:n + 1],
                                            ALU.subtract, ALU.mult).then_inc(s_xn1, 1)

            def t1_lo(b, k):
                dve.wait_ge(s_t1hi, NK * b.j + k + 1)
                nc.vector.tensor_tensor(xnT_l[:, k, :], tp[(k + 1) % 2][:, :], xnT_h[:, k, :].bitcast(F32),
                                        ALU.subtract).then_inc(s_t1lo, 1)

            def t2_lo(b, k):
                dve.wait_ge(s_t2hi, NK * b.j + k + 1)
                nc.vector.tensor_tensor(x2T_l[:, k, :], tp[k % 2][:, :], x2T_h[:, k, :].bitcast(F32),
                                        ALU.subtract).then_inc(s_t2lo, 1)

            def silu_i(b, c):
                dve.wait_ge(s_value, NK * b.j + c + 1)
                nc.vector.tensor_tensor(value[:, :], bank[QI][:, :], value[:, :], ALU.mult).then_inc(s_u, 1)

            def scan(b, c):
                dve.wait_ge(s_u, NK * b.j + c + 1)
                dve.wait_ge(s_inject, NK * b.j + c + 1)
                nc.vector.tensor_tensor(value[:, :], value[:, :], inject[:, :], ALU.mult).then_inc(s_v, 1)
                dve.wait_ge(s_v, NK * b.j + c + 1)
                if not (first(b, 0) and c == 0):
                    dve.wait_ge(s_sq, NK * b.j + c)
                state = carry[:, b.par, c:c + 1]
                nc.vector.tensor_tensor_scan(o[:, :], decay[:, :], value[:, :], state,
                                             ALU.mult, ALU.add).then_inc(s_scan, 1)
                dve.wait_ge(s_scan, NK * b.j + c + 1)
                nc.vector.tensor_copy(state, o[:, TOK - 1:TOK]).then_inc(s_carry, 1)

            def gated(b, c):
                dve.wait_ge(s_gate, NK * b.j + c + 1)
                nc.vector.tensor_tensor(gate[:, :], bank[QG][:, :], gate[:, :], ALU.mult).then_inc(s_w, 1)
                dve.wait_ge(s_w, NK * b.j + c + 1)
                nc.vector.tensor_tensor(og[:, :], o[:, :], gate[:, :], ALU.mult).then_inc(s_og, 1)
                if c > 0:
                    dve.wait_ge(s_sq, NK * b.j + c + 1)
                    if c > 1:
                        dve.wait_ge(s_osum, (NK - 1) * b.j + c - 1)
                    nc.vector.tensor_tensor(osum[:, :], osum[:, :], osq[:, :], ALU.add).then_inc(s_osum, 1)

            def og_lo(b, c):
                dve.wait_ge(s_oghi, NK * b.j + c + 1)
                nc.vector.tensor_tensor(ogT_l[:, c, :], og[:, :], ogT_h[:, c, :].bitcast(F32),
                                        ALU.subtract).then_inc(s_oglo, 1)

            def expert_inputs(b):
                for n in range(NT):
                    dve.wait_ge(s_h, NT * b.j + n + 1)
                    rest = x1[:, n, HALF:D]
                    nc.vector.tensor_tensor(rest, main_e1(n)[:, 0:REST], rest, ALU.add).then_inc(s_x1w, 1)
                    logits = h[:, n, ER:ER + E]
                    nc.vector.max(top[:, n, :], logits).then_inc(s_top, 1)
                    dve.wait_ge(s_zero, 1)
                    dve.wait_ge(s_top, NT * b.j + n + 1)
                    nc.vector.max_index(topi[:, n, :], top[:, n, :], logits).then_inc(s_topi, 1)
                nc.vector.tensor_tensor(gap[:, :], top[:, :, 0], top[:, :, 1], ALU.subtract).then_inc(s_gap, 1)
                dve.wait_ge(s_topi, NT * b.j + NT)
                nc.vector.tensor_tensor(pick[:, :, :, :],
                                        expert_no[:, :].unsqueeze(1).unsqueeze(1).broadcast_to([P, NT, 2, E]),
                                        topi[:, :, 0:2].unsqueeze(3).broadcast_to([P, NT, 2, E]),
                                        ALU.is_equal).then_inc(s_eq, 1)
                dve.wait_ge(s_eq, b.j + 1)
                dve.wait_ge(s_topw, 2 * b.j + 2)
                flat_pick = pick[:, :, :, :].rearrange("p n s e -> p (n s) e")
                nc.vector.scalar_tensor_tensor(flat_pick, flat_pick, ALPHA,
                                               topw[:, :, :].rearrange("p n s -> p (n s)").unsqueeze(2).broadcast_to([P, NT * 2, E]),
                                               ALU.mult, ALU.mult).then_inc(s_pick, 1)
                dve.wait_ge(s_pick, b.j + 1)
                nc.vector.tensor_tensor(wmat[:, :, :], pick[:, :, 0, :], pick[:, :, 1, :], ALU.add).then_inc(s_wmat, 1)
                dve.wait_ge(s_wmat, b.j + 1)
                nc.vector.tensor_tensor(hw[:, :, :].rearrange("p n (e r) -> p n e r", r=R),
                                        h[:, :, 0:ER].rearrange("p n (e r) -> p n e r", r=R),
                                        wmat[:, :, :].unsqueeze(3).broadcast_to([P, NT, E, R]),
                                        ALU.mult).then_inc(s_hw, 1)

            def hw_lo(b):
                dve.wait_ge(s_hwhi, b.j + 1)
                nc.vector.tensor_tensor(hwT_l[:, :], tp[0][:, :], hwT_h[:, :].bitcast(F32),
                                        ALU.subtract).then_inc(s_hwlo, 1)

            def final(b, n, src):
                dve.wait_ge(s_e2, NT * b.j + n + 1)
                if n >= 2:
                    dve.wait_ge(s_out[n % 2], b.j * (NT // 2 * 16) + 16)
                if n == 0:
                    dve.wait_ge(s_x1w, NT * b.j + NT)
                nc.vector.tensor_tensor(outb[:, n % 2, :], src[:, :], x1[:, n, :],
                                        ALU.add).then_inc(s_ob, 1)

            def mean_square(b):
                dve.wait_ge(s_rms, b.j + 1)
                nc.vector.tensor_scalar(ms[:, :], tp[1][:, 0:NT], 1.0 / D, EPS, ALU.mult, ALU.add).then_inc(s_ms, 1)

            def residual(b, n):
                dve.wait_ge(s_c, NT * b.j + n + 1)
                if n == 0:
                    dve.wait_ge(s_rr, b.j + 1)
                nc.vector.scalar_tensor_tensor(x1[:, n, :], main_c(n)[:, :], rr[:, n:n + 1], x[b.par][:, n, :],
                                               ALU.mult, ALU.add).then_inc(s_x1, 1)
                dve.wait_ge(s_x1, NT * b.j + n + 1)
                nc.vector.bn_stats(bn2[:, n, :], x1[:, n, :]).then_inc(s_bn2, 1)
                dve.wait_ge(s_zero, 1)
                dve.wait_ge(s_bn2, NT * b.j + n + 1)
                nc.vector.bn_aggr(mv2[:, n, :], bn2[:, n, :]).then_inc(s_mv2, 1)
                dve.wait_ge(s_mv2, NT * b.j + n + 1)
                nc.vector.tensor_scalar(ve2[:, n:n + 1], mv2[:, n, 1:2], EPS, None, ALU.add).then_inc(s_ve2, 1)

            def norm2_apply(b, n):
                dve.wait_ge(s_rstd2, NT * b.j + n + 1)
                if n == 0:
                    dve.wait_ge(s_t1, min(NK * (b.j + 2), NK * NBLK) if isinstance(b.j, int) else NK * (b.j + 2))
                nc.vector.tensor_scalar(xn[:, n, :], x1[:, n, :], mv2[:, n, 0:1], rstd2[:, n:n + 1],
                                        ALU.subtract, ALU.mult).then_inc(s_xn2, 1)

            nc.vector.memset(carry[:, :, :], 0.0).then_inc(s_zero, 1)
            norm1_stats(Block(0, 0, 0))
            norm1_apply(Block(0, 0, 0))
            split_weights(0)
            for k in range(NK):
                t1_lo(Block(0, 0, 0), k)
            dve.wait_ge(s_zero, 1)
            dve.wait_ge(s_const, 3 + E)

            def step(prev, now, nxt):
                for c in range(NK):
                    if prev is None:
                        for g in AHEAD[c]:
                            split_weights(g)
                    if prev is not None and c == 1:
                        t2_lo(prev, 2)
                    silu_i(now, c)
                    if prev is not None and c == 1:
                        t2_lo(prev, 3)
                    scan(now, c)
                    if prev is not None and c == 3:
                        hw_lo(prev)
                    gated(now, c)
                    if prev is not None and c == 0:
                        t2_lo(prev, 0)
                        t2_lo(prev, 1)
                    og_lo(now, c)
                    if prev is not None:
                        if c == 1:
                            expert_inputs(prev)
                            if nxt is not None:
                                norm1_stats(nxt)
                        if c == 2 and nxt is not None:
                            norm1_apply(nxt)
                if prev is None:
                    norm1_stats(nxt)
                    norm1_apply(nxt)
                for n in range(NT):
                    if prev is not None:
                        final(prev, n, main_e2(n))
                    if nxt is not None:
                        t1_lo(nxt, n)
                mean_square(now)
                residual(now, 0)
                for n in range(1, NT):
                    residual(now, n)
                    norm2_apply(now, n - 1)
                norm2_apply(now, NT - 1)
                if prev is not None:
                    dve.wait_ge(s_hwt, prev.j + 1)
                    for i in range(2):
                        dve.wait_ge(s_out[i], (prev.j + 1) * (NT // 2 * 16))

            flow(dve, step)
            for k in range(NK):
                t2_lo(LAST, k)
            expert_inputs(LAST)
            hw_lo(LAST)
            for n, src in enumerate((main_e2(0), main_e2(1), bank[0], bank[1])):
                final(LAST, n, src)

        @block.tensor
        def _(pe):
            def product(dst, terms, start=True, stop=True):
                for t, (lh, ll, rh, rl) in enumerate(terms):
                    nc.tensor.matmul(dst, lh, rh, start=start and t == 0, stop=False)
                    nc.tensor.matmul(dst, lh, rl, start=False, stop=False)
                    last = nc.tensor.matmul(dst, ll, rh, start=False, stop=stop and t == len(terms) - 1)
                return last

            def tok(n):
                return slice(n * P, (n + 1) * P)

            def transposes(b, k, dst, sem_xn, sem_done):
                for n in range(NT):
                    if k == 0:
                        pe.wait_ge(sem_xn, NT * b.j + n + 1)
                    last = nc.tensor.transpose(dst[:, tok(n)], xn[:, n, k * P:(k + 1) * P], ident[:, :])
                last.then_inc(sem_done, 1)

            def norm1_transposes(b, k):
                if k == 0:
                    pass
                elif k == 1 and not first(b, 0) and not first(b, 1):
                    pe.wait_ge(s_hwlo, b.j - 1)
                elif k > 1:
                    pe.wait_ge(s_t1lo, NK * b.j + k - 1)
                transposes(b, k, tp[(k + 1) % 2], s_xn1, s_t1)

            def norm2_transposes(b, k):
                if k == 1:
                    pe.wait_ge(s_ms, b.j + 1)
                elif k > 1:
                    pe.wait_ge(s_t2lo, NK * b.j + k - 1)
                transposes(b, k, tp[k % 2], s_xn2, s_t2)

            def projection(b, c, q):
                free = (s_inject, s_u, s_w)[q]
                if not (first(b, 0) and c == 0):
                    pe.wait_ge(free, NK * b.j + c)
                if first(b, 0) and q == QF:
                    pe.wait_ge(s_wlo, c + 1)
                terms = []
                if c == 0 and q == QF:
                    pe.wait_ge(s_t1lo, NK * b.j + NK)
                for k in range(NK):
                    terms.append((wproj_h[:, c, q, k, :], wproj_l[:, c, q, k, :], xnT_h[:, k, :], xnT_l[:, k, :]))
                product(bank[q][:, :], terms).then_inc(s_proj[q], 1)

            def expert_first(b, n):
                if n == 0:
                    pe.wait_ge(s_t2lo, NK * b.j + NK)
                    pe.wait_ge(s_x1, NT * b.j + NT)
                    if first(b, 0):
                        pe.wait_ge(s_wlo, len(GROUPS))
                elif n == 3:
                    pe.wait_ge(s_x1w, NT * b.j + 1)
                terms = [(x2T_h[:, k, tok(n)], x2T_l[:, k, tok(n)], wffn_h[:, k, HALF:FW], wffn_l[:, k, HALF:FW])
                         for k in range(NK)]
                product(main_e1(n)[:, 0:HALF], terms).then_inc(s_e1, 1)

            def lora_transposes(b):
                pe.wait_ge(s_hw, b.j + 1)
                pe.wait_ge(s_t2lo, NK * b.j + NK - 1)
                for n in range(NT):
                    last = nc.tensor.transpose(tp[0][0:ER, tok(n)], hw[:, n, :], ident[:, :])
                last.then_inc(s_hwt, 1)

            def expert_second(b, n):
                if n == 0:
                    pe.wait_ge(s_hwlo, b.j + 1)
                if n < 3:
                    pe.wait_ge(s_x1w, NT * b.j + n + 2)
                else:
                    pe.wait_ge(s_ob, NT * b.j + 1)
                dst = main_e2(n)
                product(dst[:, 0:D], [(hwT_h[:, tok(n)], hwT_l[:, tok(n)], wb_h[:, :], wb_l[:, :])], stop=False)
                terms = [(x2T_h[:, k, tok(n)], x2T_l[:, k, tok(n)], wffn_h[:, k, 0:HALF], wffn_l[:, k, 0:HALF])
                         for k in range(NK)]
                product(dst[:, 0:HALF], terms, start=False).then_inc(s_e2, 1)

            def rms_sums(b):
                pe.wait_ge(s_osum, (NK - 1) * (b.j + 1))
                pe.wait_ge(s_t1lo, min(NK * (b.j + 2), NK * NBLK) - 1 if isinstance(b.j, int) else NK * (b.j + 2) - 1)
                for n in range(NT):
                    last = nc.tensor.matmul(tp[1][:, n:n + 1], osum[:, tok(n)], ones[:, :], start=True, stop=True)
                last.then_inc(s_rms, 1)

            def attention_out(b, n):
                if n == 0:
                    pe.wait_ge(s_oglo, NK * (b.j + 1))
                    if first(b, 0):
                        pe.wait_ge(s_wlo, G_WO + 1)
                if n < 3:
                    if not first(b, 0):
                        pe.wait_ge(s_ob, NT * (b.j - 1) + n + 2)
                else:
                    pe.wait_ge(s_x1, NT * b.j + 1)
                terms = [(ogT_h[:, k, tok(n)], ogT_l[:, k, tok(n)], wo_h[:, k, :], wo_l[:, k, :]) for k in range(NK)]
                product(main_c(n)[:, :], terms).then_inc(s_c, 1)

            pe.wait_ge(s_const, 2)
            for k in range(NK):
                norm1_transposes(Block(0, 0, 0), k)

            def step(prev, now, nxt):
                for q in range(3):
                    projection(now, 0, q)
                if prev is not None:
                    norm2_transposes(prev, 0)
                    norm2_transposes(prev, 1)
                projection(now, 1, QF)
                if prev is not None:
                    norm2_transposes(prev, 2)
                projection(now, 1, QI)
                if prev is not None:
                    norm2_transposes(prev, 3)
                projection(now, 1, QG)
                if prev is not None:
                    for n in range(NT):
                        expert_first(prev, n)
                for q in range(3):
                    projection(now, 2, q)
                projection(now, 3, QF)
                projection(now, 3, QI)
                if prev is not None:
                    lora_transposes(prev)
                projection(now, 3, QG)
                for n in range(NT):
                    if prev is not None:
                        expert_second(prev, n)
                    if nxt is not None:
                        norm1_transposes(nxt, n)
                rms_sums(now)
                for n in range(NT):
                    attention_out(now, n)

            flow(pe, step)
            for k in range(NK):
                norm2_transposes(LAST, k)
            for n in range(NT):
                expert_first(LAST, n)
            dst = [main_e2(0), main_e2(1), bank[0], bank[1]]
            pe.wait_ge(s_x1w, NT * LAST.j + 3)
            for n in range(NT):
                terms = [(x2T_h[:, k, tok(n)], x2T_l[:, k, tok(n)], wffn_h[:, k, 0:HALF], wffn_l[:, k, 0:HALF])
                         for k in range(NK)]
                product(dst[n][:, 0:HALF], terms, stop=False)
            lora_transposes(LAST)
            pe.wait_ge(s_hwlo, NBLK)
            for n in range(NT):
                for cols, start in ((slice(0, HALF), False), (slice(HALF, D), True)):
                    last = product(dst[n][:, cols], [(hwT_h[:, tok(n)], hwT_l[:, tok(n)], wb_h[:, cols], wb_l[:, cols])],
                                   start=start)
                last.then_inc(s_e2, 1)


def kernel(L0_attn_hidden_states, L0_attn_Wi, L0_attn_Wf, L0_attn_Wg, L0_attn_Wo, L0_attn_g_norm_weight,
           L0_ffn_W, L0_ffn_gate_w, L0_ffn_A, L0_ffn_B):
    import numpy as np
    import concourse.bacc as bacc
    from concourse.bass_utils import run_bass_kernel_spmd

    P = 128
    x = np.ascontiguousarray(L0_attn_hidden_states)
    D = x.shape[-1]
    NK = D // P
    E, R, _ = L0_ffn_A.shape
    wproj = np.stack([np.asarray(w).reshape(NK, P, NK, P) for w in (L0_attn_Wf, L0_attn_Wi, L0_attn_Wg)])
    wproj = wproj.transpose(3, 2, 0, 1, 4).reshape(NK, P, 3 * NK * P)
    wo = np.asarray(L0_attn_Wo).reshape(NK, P, D).transpose(1, 0, 2)
    wffn = np.concatenate([np.asarray(L0_ffn_W).T, np.asarray(L0_ffn_A).reshape(E * R, D).T, np.asarray(L0_ffn_gate_w).T], axis=1)
    wffn = wffn.reshape(NK, P, -1).transpose(1, 0, 2)
    wb = np.asarray(L0_ffn_B).transpose(0, 2, 1).reshape(E * R, D)
    gn = np.asarray(L0_attn_g_norm_weight).reshape(NK, P).T
    arrays = {"x": x, "gn": gn, "wproj": wproj, "wo": wo, "wffn": wffn, "wb": wb}
    arrays = {f"in_{name}": np.ascontiguousarray(a) for name, a in arrays.items()}

    nc = bacc.Bacc("TRN2", target_bir_lowering=False, num_devices=1)
    ins = [nc.dram_tensor(name, a.shape, mybir.dt.from_np(a.dtype), kind="ExternalInput").ap() for name, a in arrays.items()]
    out = nc.dram_tensor("out", x.shape, mybir.dt.from_np(x.dtype), kind="ExternalOutput").ap()
    hgrn_lora_moe(nc, *ins, out)
    return run_bass_kernel_spmd(nc, [arrays], core_ids=[0]).results[0]["out"]
```

```python
from collections import namedtuple
from contextlib import ExitStack

import concourse.bass as bass
from concourse import mybir

Block = namedtuple("Block", "j par tb")


def hgrn_lora_moe(nc, x_in, gn_in, wproj_in, wo_in, wffn_in, wb_in, out):
    F32, F32R, U32 = mybir.dt.float32, mybir.dt.float32r, mybir.dt.uint32
    ALU, ACT = mybir.AluOpType, mybir.ActivationFunctionType

    P = 128
    NSEQ, SEQ, D = x_in.shape
    NT = 4
    TOK = NT * P
    NBLK = NSEQ * SEQ // TOK
    NK = D // P
    ER = wb_in.shape[0]
    FW = wffn_in.shape[2]
    E = FW - D - ER
    R = ER // E
    HALF = FW // 2
    REST = D - HALF
    EPS, ALPHA = 1e-5, 16.0
    PROJ = 3 * NK * P
    QF, QI, QG = range(3)

    x_v = x_in.rearrange("b (t n p) d -> b t p n d", n=NT, p=P)
    out_v = out.rearrange("b (t n p) d -> b t n p d", n=NT, p=P)

    ctx = ExitStack()
    with ctx:
        def sb(name, shape, dt=F32):
            return ctx.enter_context(nc.sbuf_tensor(name, shape, dt))

        def pb(name):
            return ctx.enter_context(nc.psum_tensor(name, [P, 512], F32))

        def sem(name):
            return ctx.enter_context(nc.semaphore(name))

        wproj_h = sb("wproj_h", [P, NK, 3, NK, P], F32R)
        wproj_l = sb("wproj_l", [P, NK, 3, NK, P], F32R)
        wo_h = sb("wo_h", [P, NK, D], F32R)
        wo_l = sb("wo_l", [P, NK, D], F32R)
        wffn_h = sb("wffn_h", [P, NK, FW], F32R)
        wffn_l = sb("wffn_l", [P, NK, FW], F32R)
        wb_h = sb("wb_h", [ER, D], F32R)
        wb_l = sb("wb_l", [ER, D], F32R)
        gn = sb("gn", [P, NK])
        x = [sb(f"x_seq{i}", [P, NT, D]) for i in range(2)]
        x1 = sb("x1", [P, NT, D])
        xn = sb("xn", [P, NT, D])
        outb = sb("outb", [P, 2, D])
        stage = sb("stage", [P, NK, 3 * P])
        xnT_h = sb("xnT_h", [P, NK, TOK], F32R)
        xnT_l = sb("xnT_l", [P, NK, TOK], F32R)
        x2T_h = sb("x2T_h", [P, NK, TOK], F32R)
        x2T_l = sb("x2T_l", [P, NK, TOK], F32R)
        ogT_h = sb("ogT_h", [P, NK, TOK], F32R)
        ogT_l = sb("ogT_l", [P, NK, TOK], F32R)
        decay = sb("decay", [P, TOK])
        inject = sb("inject", [P, TOK])
        value = sb("value", [P, TOK])
        gate = sb("gate", [P, TOK])
        o = sb("o", [P, TOK])
        og = sb("og", [P, TOK])
        osq = sb("osq", [P, TOK])
        osum = sb("osum", [P, TOK])
        carry = sb("carry", [P, NSEQ, NK])
        h = sb("h", [P, NT, ER + E])
        top = sb("top", [P, NT, 8])
        topi = sb("topi", [P, NT, 8], U32)
        gap = sb("gap", [P, NT])
        topw = sb("topw", [P, NT, 2])
        pick = sb("pick", [P, NT, 2, E])
        wmat = sb("wmat", [P, NT, E])
        hw = sb("hw", [P, NT, ER])
        hwT_h = sb("hwT_h", [ER, TOK], F32R)
        hwT_l = sb("hwT_l", [ER, TOK], F32R)
        bn1, mv1, ve1, rstd1 = (sb(n, s) for n, s in (("bn1", [P, NT, 6]), ("mv1", [P, NT, 2]), ("ve1", [P, NT]), ("rstd1", [P, NT])))
        bn2, mv2, ve2, rstd2 = (sb(n, s) for n, s in (("bn2", [P, NT, 6]), ("mv2", [P, NT, 2]), ("ve2", [P, NT]), ("rstd2", [P, NT])))
        ms, rr = sb("ms", [P, NT]), sb("rr", [P, NT])
        ident = sb("ident", [P, P])
        ones = sb("ones", [P, 1])
        minus_half = sb("minus_half", [P, NT])
        expert_no = sb("expert_no", [P, E])

        bank = [pb(n) for n in ("psum_f", "psum_i", "psum_g")]
        tp = [pb("psum_t0"), pb("psum_t1")]
        main = [pb(f"psum_m{i}") for i in range(3)]

        def main_e1(n):
            return main[n % 3]

        def main_e2(n):
            return main[(NT + n) % 3]

        def main_c(n):
            return main[(2 * NT + n) % 3]

        T1_FIRST = [tp[1], tp[0], main[0], main[1]]

        def t1_bank(n):
            return tp[(n + 1) % 2]

        def tile_of(featT, n):
            return featT[:, :, n * P:(n + 1) * P]

        def by_chunk(psum):
            return psum[:, :].rearrange("p (k t) -> p k t", t=P)

        s_x = [sem("x_seq0_loaded"), sem("x_seq1_loaded")]
        s_xt = [sem(f"x_tile{n}_loaded") for n in range(NT)]
        s_gn = sem("gn_loaded")
        s_out = [sem("out0_stored"), sem("out1_stored")]
        s_const = sem("constants_made")
        s_ident = sem("ident_zeroed")
        s_gnw = sem("wo_scaled")
        s_table = sem("sigmoid_table_loaded")
        s_whi, s_wlo, s_wlo_pool = sem("weights_hi"), sem("weights_lo"), sem("weights_lo_by_pool")
        s_proj = [sem("f_done"), sem("i_done"), sem("g_done")]
        s_t1, s_t2, s_hwt = sem("t1_done"), sem("t2_done"), sem("hwt_done")
        s_e1, s_e2, s_rms, s_c = sem("e1_done"), sem("e2_done"), sem("rms_done"), sem("c_done")
        s_decay, s_inject, s_value, s_gate = sem("decay_ready"), sem("inject_ready"), sem("value_ready"), sem("gate_ready")
        s_sq, s_oghi = sem("osq_ready"), sem("og_hi")
        s_t1hi, s_t2hi, s_hwhi = sem("t1_hi"), sem("t2_hi"), sem("hw_hi")
        s_h, s_topw = sem("h_copied"), sem("topw_ready")
        s_u, s_v, s_scan, s_carry = sem("silu_i"), sem("scan_input"), sem("scan_done"), sem("carry_saved")
        s_w, s_og, s_oglo, s_osum = sem("silu_g"), sem("og_ready"), sem("og_lo"), sem("osum_ready")
        s_t1lo, s_t2lo, s_hwlo = sem("t1_lo"), sem("t2_lo"), sem("hw_lo")
        s_x1w, s_top, s_topi, s_gap = sem("x1_rest"), sem("top_ready"), sem("topi_ready"), sem("gap_ready")
        s_eq, s_pick, s_wmat, s_hw = sem("eq_ready"), sem("pick_ready"), sem("wmat_ready"), sem("hw_ready")
        s_ob, s_ms, s_x1 = sem("out_ready"), sem("ms_ready"), sem("x1_ready")
        s_bn1, s_mv1, s_ve1, s_xn1 = sem("bn1_done"), sem("mv1_done"), sem("ve1_ready"), sem("xn1_ready")
        s_bn2, s_mv2, s_ve2, s_xn2 = sem("bn2_done"), sem("mv2_done"), sem("ve2_ready"), sem("xn2_ready")
        s_zero = sem("carry_zeroed")
        s_rstd1, s_rr, s_rstd2 = sem("rstd1_ready"), sem("rr_ready"), sem("rstd2_ready")

        def flow(eng, step):
            step(None, Block(0, 0, 0), Block(1, 1, 0))
            with eng.Fori(0, (NBLK - 2) // 2) as k:
                step(Block(2 * k, 0, k), Block(2 * k + 1, 1, k), Block(2 * k + 2, 0, k + 1))
                step(Block(2 * k + 1, 1, k), Block(2 * k + 2, 0, k + 1), Block(2 * k + 3, 1, k + 1))
            step(Block(NBLK - 2, 0, NBLK // 2 - 1), Block(NBLK - 1, 1, NBLK // 2 - 1), None)

        def first(b, j):
            return isinstance(b.j, int) and b.j == j

        LAST = Block(NBLK - 1, 1, NBLK // 2 - 1)

        AREAS = [ap[:, :, :].rearrange("p n d -> p (n d)") for ap in (x1, x[1], stage, outb, xn)]
        GROUPS = []

        def flat(ap):
            return ap.rearrange("p k n -> p (k n)")

        def group(area, src, hi, lo, at=0):
            GROUPS.append((src, AREAS[area][:, at:at + src.shape[1]], hi, lo, area))

        QW = NK * P
        for q in range(3):
            group(0, wproj_in[0][:, q * QW:(q + 1) * QW], flat(wproj_h[:, 0, q]), flat(wproj_l[:, 0, q]), at=q * QW)
        for c, area in ((1, 1), (2, 2), (3, 0)):
            group(area, wproj_in[c], wproj_h[:, c].rearrange("p q k n -> p (q k n)"),
                  wproj_l[:, c].rearrange("p q k n -> p (q k n)"))
        G1, G2, G3, G_FFN0, G_WO, G_FFN1, G_B = range(3, 10)
        lo_half, hi_half = slice(0, NK // 2), slice(NK // 2, NK)
        group(2, flat(wffn_in[:, lo_half, :]), flat(wffn_h[:, lo_half, :]), flat(wffn_l[:, lo_half, :]))
        group(4, flat(wo_in), flat(wo_h[:, :, :]), flat(wo_l[:, :, :]))
        group(2, flat(wffn_in[:, hi_half, :]), flat(wffn_h[:, hi_half, :]), flat(wffn_l[:, hi_half, :]))
        group(3, wb_in, wb_h[:, :], wb_l[:, :])
        AFTER = {G3: 2, G_FFN0: G2}
        s_stage = [sem(f"weights{g}_loaded") for g in range(len(GROUPS))]
        BY_POOL = (G_FFN0, G_WO, G_FFN1, G_B)

        block = ctx.enter_context(nc.Block())

        @block.sync
        def _(sp):
            def load_x(b):
                sp.dma_start(x[b.par][:, :, :], x_v[b.par, b.tb]).then_inc(s_x[b.par], 16)

            def store_out(b):
                for n in range(NT):
                    sp.wait_ge(s_ob, NT * b.j + n + 1)
                    sp.dma_start(out_v[b.par, b.tb, n], outb[:, n % 2, :]).then_inc(s_out[n % 2], 16)

            def load_x_tile(n):
                sp.dma_start(x[0][:, n, :], x_v[0, 0][:, n, :]).then_inc(s_xt[n], 16)

            def load_group(g):
                if g in AFTER:
                    sp.wait_ge(s_wlo, AFTER[g] + 1)
                sp.dma_start(GROUPS[g][1], GROUPS[g][0]).then_inc(s_stage[g], 16)

            load_x_tile(0)
            load_x_tile(1)
            load_group(0)
            load_x_tile(2)
            load_x_tile(3)
            for g in (1, 2, G1, G2):
                load_group(g)
            sp.dma_start(gn[:, :], gn_in).then_inc(s_gn, 16)
            load_group(G_B)
            load_group(G3)
            sp.wait_ge(s_t1, NT)
            load_group(G_WO)
            sp.wait_ge(s_wlo, G1 + 1)
            load_x(Block(1, 1, 0))
            load_group(G_FFN0)
            sp.wait_ge(s_wlo_pool, 1)
            load_group(G_FFN1)

            def step(prev, now, nxt):
                if prev is not None:
                    if nxt is not None:
                        sp.wait_ge(s_x1, NT * now.j)
                        load_x(nxt)
                    store_out(prev)

            flow(sp, step)
            store_out(LAST)
            for i in range(2):
                sp.wait_ge(s_out[i], NBLK * NT // 2 * 16)

        @block.gpsimd
        def _(pool):
            nc.gpsimd.memset(ident[:, :], 0.0).then_inc(s_ident, 1)
            pool.wait_ge(s_ident, 1)
            nc.gpsimd.affine_select(out=ident[:, :], in_=ident[:, :], compare_op=ALU.not_equal, fill=1.0,
                                    base=0, pattern=[[-1, P]], channel_multiplier=1).then_inc(s_const, 1)
            nc.gpsimd.memset(ones[:, :], 1.0).then_inc(s_const, 1)
            nc.gpsimd.memset(minus_half[:, :], -0.5).then_inc(s_const, 1)
            for e in range(E):
                nc.gpsimd.memset(expert_no[:, e:e + 1], float(e)).then_inc(s_const, 1)
            pool.wait_ge(s_const, 3)

            def norm1(b):
                pool.wait_ge(s_ve1, 2 * b.j + NT)
                nc.gpsimd.tensor_tensor(rstd1[:, :], ve1[:, :], minus_half[:, :], ALU.pow).then_inc(s_rstd1, 1)

            def split_weights(g):
                _, raw, hi, lo, _ = GROUPS[g]
                if g == G_WO:
                    pool.wait_ge(s_stage[g], 16)
                    pool.wait_ge(s_gn, 16)
                    for k in range(NK):
                        part = raw[:, k * D:(k + 1) * D]
                        nc.gpsimd.tensor_scalar(part, part, gn[:, k:k + 1], 1.0, ALU.mult, ALU.mult).then_inc(s_gnw, 1)
                    pool.wait_ge(s_gnw, NK)
                pool.wait_ge(s_whi, g + 1)
                nc.gpsimd.tensor_tensor(lo, raw, hi.bitcast(F32), ALU.subtract).then_inc(s_wlo_pool, 1)

            for n in range(NT):
                pool.wait_ge(s_ve1, n + 1)
                nc.gpsimd.tensor_tensor(rstd1[:, n:n + 1], ve1[:, n:n + 1], minus_half[:, 0:1],
                                        ALU.pow).then_inc(s_rstd1, 1)

            split_weights(G_FFN0)
            split_weights(G_WO)

            def step(prev, now, nxt):
                if nxt is not None:
                    norm1(nxt)
                if prev is None:
                    split_weights(G_FFN1)
                    split_weights(G_B)
                pool.wait_ge(s_ms, now.j + 1)
                nc.gpsimd.tensor_tensor(rr[:, :], ms[:, :], minus_half[:, :], ALU.pow).then_inc(s_rr, 1)
                for n in range(NT):
                    pool.wait_ge(s_ve2, NT * now.j + n + 1)
                    nc.gpsimd.tensor_tensor(rstd2[:, n:n + 1], ve2[:, n:n + 1], minus_half[:, 0:1],
                                            ALU.pow).then_inc(s_rstd2, 1)

            flow(pool, step)

        @block.scalar
        def _(act):
            def split_weights(g):
                _, raw, hi, _, _ = GROUPS[g]
                if g == G_WO:
                    act.wait_ge(s_gnw, NK)
                else:
                    act.wait_ge(s_stage[g], 16)
                nc.scalar.activation(hi, raw, ACT.Copy).then_inc(s_whi, 1)

            def t1_hi(b, n, src):
                act.wait_ge(s_t1, NT * b.j + n + 1)
                nc.scalar.activation(tile_of(xnT_h, n), by_chunk(src), ACT.Copy).then_inc(s_t1hi, 1)

            def t2_hi(b, n):
                act.wait_ge(s_t2, NT * b.j + n + 1)
                nc.scalar.activation(tile_of(x2T_h, n), by_chunk(tp[n % 2]), ACT.Copy).then_inc(s_t2hi, 1)

            def forget(b, c):
                act.wait_ge(s_proj[QF], NK * b.j + c + 1)
                if not (first(b, 0) and c == 0):
                    act.wait_ge(s_scan, NK * b.j + c)
                nc.scalar.activation(decay[:, :], bank[QF][:, :], ACT.Sigmoid).then_inc(s_decay, 1)
                nc.scalar.activation(inject[:, :], bank[QF][:, :], ACT.Sigmoid, scale=-1.0).then_inc(s_inject, 1)

            def put(b, c):
                act.wait_ge(s_proj[QI], NK * b.j + c + 1)
                nc.scalar.activation(value[:, :], bank[QI][:, :], ACT.Sigmoid).then_inc(s_value, 1)

            def output_gate(b, c):
                act.wait_ge(s_proj[QG], NK * b.j + c + 1)
                if not (first(b, 0) and c == 0):
                    act.wait_ge(s_og, NK * b.j + c)
                nc.scalar.activation(gate[:, :], bank[QG][:, :], ACT.Sigmoid).then_inc(s_gate, 1)

            def square(b, c):
                act.wait_ge(s_scan, NK * b.j + c + 1)
                if c == 0:
                    if not first(b, 0):
                        act.wait_ge(s_rms, b.j)
                    dst = osum
                else:
                    if c == 1 and not first(b, 0):
                        act.wait_ge(s_osum, (NK - 1) * b.j)
                    elif c > 1:
                        act.wait_ge(s_osum, (NK - 1) * b.j + c - 1)
                    dst = osq
                nc.scalar.activation(dst[:, :], o[:, :], ACT.Square).then_inc(s_sq, 1)

            def og_hi(b, c):
                act.wait_ge(s_og, NK * b.j + c + 1)
                if c == 0 and not first(b, 0):
                    act.wait_ge(s_c, NT * b.j)
                nc.scalar.activation(ogT_h[:, c, :], og[:, :], ACT.Copy).then_inc(s_oghi, 1)

            def expert_inputs(b):
                if b is LAST:
                    t2_hi(b, 0)
                    t2_hi(b, 1)
                for n in range(NT):
                    if b is LAST and n + 2 < NT:
                        t2_hi(b, n + 2)
                    act.wait_ge(s_e1, NT * b.j + n + 1)
                    nc.scalar.activation(h[:, n, :], main_e1(n)[:, REST:HALF], ACT.Copy).then_inc(s_h, 1)
                act.wait_ge(s_gap, b.j + 1)
                nc.scalar.activation(topw[:, :, 0], gap[:, :], ACT.Sigmoid).then_inc(s_topw, 1)
                nc.scalar.activation(topw[:, :, 1], gap[:, :], ACT.Sigmoid, scale=-1.0).then_inc(s_topw, 1)

            def hw_hi(b):
                act.wait_ge(s_hwt, b.j + 1)
                nc.scalar.activation(hwT_h[:, :], tp[0][:, :], ACT.Copy).then_inc(s_hwhi, 1)

            act.wait_ge(s_const, 3)
            nc.scalar.activation(topw[:, :, 0], minus_half[:, :], ACT.Sigmoid).then_inc(s_table, 1)
            for n in range(NT):
                if n < 3:
                    split_weights(n)
                t1_hi(Block(0, 0, 0), n, T1_FIRST[n])

            def step(prev, now, nxt):
                if prev is None:
                    split_weights(G1)
                    split_weights(G2)
                for c in range(NK):
                    forget(now, c)
                    if prev is None and c > 0:
                        split_weights((G_FFN0, G_WO, G_FFN1)[c - 1])
                    if prev is not None and c == 1:
                        t2_hi(prev, 2)
                    put(now, c)
                    if prev is not None and c == 1:
                        t2_hi(prev, 3)
                    if prev is not None and c == 3:
                        hw_hi(prev)
                    if prev is None and c == 0:
                        split_weights(G3)
                    if prev is None and c == 3:
                        split_weights(G_B)
                    output_gate(now, c)
                    square(now, c)
                    if prev is not None and c == 0:
                        t2_hi(prev, 0)
                        t2_hi(prev, 1)
                    og_hi(now, c)
                    if prev is not None and c == 1:
                        expert_inputs(prev)
                if nxt is not None:
                    for n in range(NT):
                        t1_hi(nxt, n, t1_bank(n))
                if prev is not None:
                    act.wait_ge(s_hw, prev.j + 1)

            flow(act, step)
            expert_inputs(LAST)
            hw_hi(LAST)

        @block.vector
        def _(dve):
            def split_weights(g):
                _, raw, hi, lo, _ = GROUPS[g]
                dve.wait_ge(s_whi, g + 1)
                nc.vector.tensor_tensor(lo, raw, hi.bitcast(F32), ALU.subtract).then_inc(s_wlo, 1)

            def norm1_stats(b):
                dve.wait_ge(s_x[b.par], 16 * (b.tb + b.par))
                for n in range(NT):
                    if n > 0:
                        dve.wait_ge(s_bn1, NT * b.j + n)
                    nc.vector.bn_stats(bn1[:, n, :], x[b.par][:, n, :]).then_inc(s_bn1, 1)
                    if n > 0:
                        nc.vector.bn_aggr(mv1[:, n - 1, :], bn1[:, n - 1, :]).then_inc(s_mv1, 1)
                dve.wait_ge(s_mv1, NT * b.j + NT - 1)
                dve.wait_ge(s_bn1, NT * b.j + NT)
                nc.vector.tensor_scalar(ve1[:, 0:NT - 1], mv1[:, 0:NT - 1, 1], EPS, None, ALU.add).then_inc(s_ve1, 1)
                nc.vector.bn_aggr(mv1[:, NT - 1, :], bn1[:, NT - 1, :]).then_inc(s_mv1, 1)
                dve.wait_ge(s_mv1, NT * b.j + NT)
                nc.vector.tensor_scalar(ve1[:, NT - 1:NT], mv1[:, NT - 1, 1:2], EPS, None, ALU.add).then_inc(s_ve1, 1)

            def norm1_apply(b):
                dve.wait_ge(s_rstd1, b.j + NT)
                if not first(b, 1):
                    dve.wait_ge(s_t2, NT * (b.j - 1))
                for n in range(NT):
                    nc.vector.tensor_scalar(xn[:, n, :], x[b.par][:, n, :], mv1[:, n, 0:1], rstd1[:, n:n + 1],
                                            ALU.subtract, ALU.mult).then_inc(s_xn1, 1)

            def t1_lo(b, n, src):
                dve.wait_ge(s_t1hi, NT * b.j + n + 1)
                nc.vector.tensor_tensor(tile_of(xnT_l, n), by_chunk(src), tile_of(xnT_h, n).bitcast(F32),
                                        ALU.subtract).then_inc(s_t1lo, 1)

            def t2_lo(b, n):
                dve.wait_ge(s_t2hi, NT * b.j + n + 1)
                nc.vector.tensor_tensor(tile_of(x2T_l, n), by_chunk(tp[n % 2]), tile_of(x2T_h, n).bitcast(F32),
                                        ALU.subtract).then_inc(s_t2lo, 1)

            def silu_i(b, c):
                dve.wait_ge(s_value, NK * b.j + c + 1)
                nc.vector.tensor_tensor(value[:, :], bank[QI][:, :], value[:, :], ALU.mult).then_inc(s_u, 1)

            def scan(b, c):
                dve.wait_ge(s_u, NK * b.j + c + 1)
                dve.wait_ge(s_inject, NK * b.j + c + 1)
                nc.vector.tensor_tensor(value[:, :], value[:, :], inject[:, :], ALU.mult).then_inc(s_v, 1)
                dve.wait_ge(s_v, NK * b.j + c + 1)
                if not (first(b, 0) and c == 0):
                    dve.wait_ge(s_sq, NK * b.j + c)
                state = carry[:, b.par, c:c + 1]
                nc.vector.tensor_tensor_scan(o[:, :], decay[:, :], value[:, :], state,
                                             ALU.mult, ALU.add).then_inc(s_scan, 1)
                dve.wait_ge(s_scan, NK * b.j + c + 1)
                nc.vector.tensor_copy(state, o[:, TOK - 1:TOK]).then_inc(s_carry, 1)

            def gated(b, c):
                dve.wait_ge(s_gate, NK * b.j + c + 1)
                nc.vector.tensor_tensor(gate[:, :], bank[QG][:, :], gate[:, :], ALU.mult).then_inc(s_w, 1)
                dve.wait_ge(s_w, NK * b.j + c + 1)
                nc.vector.tensor_tensor(og[:, :], o[:, :], gate[:, :], ALU.mult).then_inc(s_og, 1)
                if c > 0:
                    dve.wait_ge(s_sq, NK * b.j + c + 1)
                    if c > 1:
                        dve.wait_ge(s_osum, (NK - 1) * b.j + c - 1)
                    nc.vector.tensor_tensor(osum[:, :], osum[:, :], osq[:, :], ALU.add).then_inc(s_osum, 1)

            def og_lo(b, c):
                dve.wait_ge(s_oghi, NK * b.j + c + 1)
                nc.vector.tensor_tensor(ogT_l[:, c, :], og[:, :], ogT_h[:, c, :].bitcast(F32),
                                        ALU.subtract).then_inc(s_oglo, 1)

            def expert_inputs(b):
                for n in range(NT):
                    if b is LAST and n + 2 < NT:
                        t2_lo(b, n + 2)
                    dve.wait_ge(s_h, NT * b.j + n + 1)
                    rest = x1[:, n, HALF:D]
                    nc.vector.tensor_tensor(rest, main_e1(n)[:, 0:REST], rest, ALU.add).then_inc(s_x1w, 1)
                    logits = h[:, n, ER:ER + E]
                    nc.vector.max(top[:, n, :], logits).then_inc(s_top, 1)
                    dve.wait_ge(s_zero, 1)
                    dve.wait_ge(s_top, NT * b.j + n + 1)
                    nc.vector.max_index(topi[:, n, :], top[:, n, :], logits).then_inc(s_topi, 1)
                nc.vector.tensor_tensor(gap[:, :], top[:, :, 0], top[:, :, 1], ALU.subtract).then_inc(s_gap, 1)
                dve.wait_ge(s_topi, NT * b.j + NT)
                nc.vector.tensor_tensor(pick[:, :, :, :],
                                        expert_no[:, :].unsqueeze(1).unsqueeze(1).broadcast_to([P, NT, 2, E]),
                                        topi[:, :, 0:2].unsqueeze(3).broadcast_to([P, NT, 2, E]),
                                        ALU.is_equal).then_inc(s_eq, 1)
                dve.wait_ge(s_eq, b.j + 1)
                dve.wait_ge(s_topw, 2 * b.j + 2)
                flat_pick = pick[:, :, :, :].rearrange("p n s e -> p (n s) e")
                nc.vector.scalar_tensor_tensor(flat_pick, flat_pick, ALPHA,
                                               topw[:, :, :].rearrange("p n s -> p (n s)").unsqueeze(2).broadcast_to([P, NT * 2, E]),
                                               ALU.mult, ALU.mult).then_inc(s_pick, 1)
                dve.wait_ge(s_pick, b.j + 1)
                nc.vector.tensor_tensor(wmat[:, :, :], pick[:, :, 0, :], pick[:, :, 1, :], ALU.add).then_inc(s_wmat, 1)
                dve.wait_ge(s_wmat, b.j + 1)
                nc.vector.tensor_tensor(hw[:, :, :].rearrange("p n (e r) -> p n e r", r=R),
                                        h[:, :, 0:ER].rearrange("p n (e r) -> p n e r", r=R),
                                        wmat[:, :, :].unsqueeze(3).broadcast_to([P, NT, E, R]),
                                        ALU.mult).then_inc(s_hw, 1)

            def hw_lo(b):
                dve.wait_ge(s_hwhi, b.j + 1)
                nc.vector.tensor_tensor(hwT_l[:, :], tp[0][:, :], hwT_h[:, :].bitcast(F32),
                                        ALU.subtract).then_inc(s_hwlo, 1)

            def final(b, n, src):
                dve.wait_ge(s_e2, NT * b.j + n + 1)
                if n >= 2:
                    dve.wait_ge(s_out[n % 2], b.j * (NT // 2 * 16) + 16)
                if n == 0:
                    dve.wait_ge(s_x1w, NT * b.j + NT)
                nc.vector.tensor_tensor(outb[:, n % 2, :], src[:, :], x1[:, n, :],
                                        ALU.add).then_inc(s_ob, 1)

            def mean_square(b):
                dve.wait_ge(s_rms, b.j + 1)
                nc.vector.tensor_scalar(ms[:, :], tp[1][:, 0:NT], 1.0 / D, EPS, ALU.mult, ALU.add).then_inc(s_ms, 1)

            def residual(b, n):
                dve.wait_ge(s_c, NT * b.j + n + 1)
                if n == 0:
                    dve.wait_ge(s_rr, b.j + 1)
                nc.vector.scalar_tensor_tensor(x1[:, n, :], main_c(n)[:, :], rr[:, n:n + 1], x[b.par][:, n, :],
                                               ALU.mult, ALU.add).then_inc(s_x1, 1)
                dve.wait_ge(s_x1, NT * b.j + n + 1)
                nc.vector.bn_stats(bn2[:, n, :], x1[:, n, :]).then_inc(s_bn2, 1)
                dve.wait_ge(s_zero, 1)
                dve.wait_ge(s_bn2, NT * b.j + n + 1)
                nc.vector.bn_aggr(mv2[:, n, :], bn2[:, n, :]).then_inc(s_mv2, 1)
                dve.wait_ge(s_mv2, NT * b.j + n + 1)
                nc.vector.tensor_scalar(ve2[:, n:n + 1], mv2[:, n, 1:2], EPS, None, ALU.add).then_inc(s_ve2, 1)

            def norm2_apply(b, n):
                dve.wait_ge(s_rstd2, NT * b.j + n + 1)
                if n == 0:
                    dve.wait_ge(s_t1, NT * NBLK if first(b, NBLK - 1) else NT * (b.j + 2))
                nc.vector.tensor_scalar(xn[:, n, :], x1[:, n, :], mv2[:, n, 0:1], rstd2[:, n:n + 1],
                                        ALU.subtract, ALU.mult).then_inc(s_xn2, 1)

            nc.vector.memset(carry[:, :, :], 0.0).then_inc(s_zero, 1)

            def first_norm_stats(n):
                dve.wait_ge(s_xt[n], 16)
                nc.vector.bn_stats(bn1[:, n, :], x[0][:, n, :]).then_inc(s_bn1, 1)
                dve.wait_ge(s_bn1, n + 1)
                nc.vector.bn_aggr(mv1[:, n, :], bn1[:, n, :]).then_inc(s_mv1, 1)
                dve.wait_ge(s_mv1, n + 1)
                nc.vector.tensor_scalar(ve1[:, n:n + 1], mv1[:, n, 1:2], EPS, None, ALU.add).then_inc(s_ve1, 1)

            def first_norm_apply(n):
                dve.wait_ge(s_rstd1, n + 1)
                nc.vector.tensor_scalar(xn[:, n, :], x[0][:, n, :], mv1[:, n, 0:1], rstd1[:, n:n + 1],
                                        ALU.subtract, ALU.mult).then_inc(s_xn1, 1)

            first_norm_stats(0)
            for n in range(1, NT):
                first_norm_stats(n)
                first_norm_apply(n - 1)
            split_weights(0)
            first_norm_apply(NT - 1)
            for n in range(NT):
                t1_lo(Block(0, 0, 0), n, T1_FIRST[n])
            split_weights(1)
            split_weights(2)
            dve.wait_ge(s_zero, 1)
            dve.wait_ge(s_const, 3 + E)

            def step(prev, now, nxt):
                if prev is None:
                    split_weights(G1)
                    split_weights(G2)
                for c in range(NK):
                    if prev is not None and c == 1:
                        t2_lo(prev, 2)
                    silu_i(now, c)
                    if prev is not None and c == 1:
                        t2_lo(prev, 3)
                    if prev is not None and c == 3:
                        hw_lo(prev)
                    scan(now, c)
                    if prev is None and c == 0:
                        split_weights(G3)
                    gated(now, c)
                    if prev is not None and c == 0:
                        t2_lo(prev, 0)
                        t2_lo(prev, 1)
                    og_lo(now, c)
                    if c == 1:
                        if prev is not None:
                            expert_inputs(prev)
                        if nxt is not None:
                            norm1_stats(nxt)
                    if c == 2 and nxt is not None:
                        norm1_apply(nxt)
                for n in range(NT):
                    if prev is not None:
                        final(prev, n, main_e2(n))
                    if nxt is not None:
                        t1_lo(nxt, n, t1_bank(n))
                mean_square(now)
                residual(now, 0)
                for n in range(1, NT):
                    residual(now, n)
                    norm2_apply(now, n - 1)
                    if nxt is None and n > 1:
                        t2_lo(now, n - 2)
                norm2_apply(now, NT - 1)
                if prev is not None:
                    dve.wait_ge(s_hwt, prev.j + 1)
                    for i in range(2):
                        dve.wait_ge(s_out[i], (prev.j + 1) * (NT // 2 * 16))

            flow(dve, step)
            expert_inputs(LAST)
            hw_lo(LAST)
            for n, src in enumerate((main_e2(0), main_e2(1), bank[0], bank[1])):
                final(LAST, n, src)

        @block.tensor
        def _(pe):
            def product(dst, terms, start=True, stop=True):
                for t, (lh, ll, rh, rl) in enumerate(terms):
                    nc.tensor.matmul(dst, lh, rh, start=start and t == 0, stop=False)
                    nc.tensor.matmul(dst, lh, rl, start=False, stop=False)
                    last = nc.tensor.matmul(dst, ll, rh, start=False, stop=stop and t == len(terms) - 1)
                return last

            def tok(n):
                return slice(n * P, (n + 1) * P)

            def transposes(b, n, dst, sem_xn, sem_done):
                pe.wait_ge(sem_xn, NT * b.j + n + 1)
                for k in range(NK):
                    last = nc.tensor.transpose(dst[:, k * P:(k + 1) * P], xn[:, n, k * P:(k + 1) * P], ident[:, :])
                last.then_inc(sem_done, 1)

            def norm1_transposes(b, n):
                if n == 1 and not first(b, 1):
                    pe.wait_ge(s_hwlo, b.j - 1)
                elif n > 1:
                    pe.wait_ge(s_t1lo, NT * b.j + n - 1)
                transposes(b, n, tp[(n + 1) % 2], s_xn1, s_t1)

            def norm2_transposes(b, n):
                if n == 1:
                    pe.wait_ge(s_ms, b.j + 1)
                elif n > 1:
                    pe.wait_ge(s_t2lo, NT * b.j + n - 1)
                transposes(b, n, tp[n % 2], s_xn2, s_t2)

            def projection(b, c, q):
                free = (s_inject, s_u, s_w)[q]
                if not (first(b, 0) and c == 0):
                    pe.wait_ge(free, NK * b.j + c)
                if first(b, 0) and c == 0 and q > 0:
                    pe.wait_ge(s_wlo, q + 1)
                elif first(b, 0) and q == QF:
                    pe.wait_ge(s_wlo, (1, G1 + 1, G2 + 1, G3 + 1)[c])
                terms = []
                if c == 0 and q == QF:
                    pe.wait_ge(s_t1lo, NT * b.j + NT)
                for k in range(NK):
                    terms.append((wproj_h[:, c, q, k, :], wproj_l[:, c, q, k, :], xnT_h[:, k, :], xnT_l[:, k, :]))
                product(bank[q][:, :], terms).then_inc(s_proj[q], 1)

            def expert_first(b, n):
                pe.wait_ge(s_t2lo, NT * b.j + n + 1)
                if n == 0:
                    pe.wait_ge(s_x1, NT * b.j + NT)
                    if first(b, 0):
                        pe.wait_ge(s_wlo_pool, len(BY_POOL))
                elif n == 3:
                    pe.wait_ge(s_x1w, NT * b.j + 1)
                terms = [(x2T_h[:, k, tok(n)], x2T_l[:, k, tok(n)], wffn_h[:, k, HALF:FW], wffn_l[:, k, HALF:FW])
                         for k in range(NK)]
                product(main_e1(n)[:, 0:HALF], terms).then_inc(s_e1, 1)

            def lora_transposes(b):
                pe.wait_ge(s_hw, b.j + 1)
                pe.wait_ge(s_t2lo, NT * b.j + NT - 1)
                for n in range(NT):
                    last = nc.tensor.transpose(tp[0][0:ER, tok(n)], hw[:, n, :], ident[:, :])
                last.then_inc(s_hwt, 1)

            def expert_second(b, n):
                if n == 0:
                    pe.wait_ge(s_hwlo, b.j + 1)
                if n < 3:
                    pe.wait_ge(s_x1w, NT * b.j + n + 2)
                else:
                    pe.wait_ge(s_ob, NT * b.j + 1)
                dst = main_e2(n)
                product(dst[:, 0:D], [(hwT_h[:, tok(n)], hwT_l[:, tok(n)], wb_h[:, :], wb_l[:, :])], stop=False)
                terms = [(x2T_h[:, k, tok(n)], x2T_l[:, k, tok(n)], wffn_h[:, k, 0:HALF], wffn_l[:, k, 0:HALF])
                         for k in range(NK)]
                product(dst[:, 0:HALF], terms, start=False).then_inc(s_e2, 1)

            def rms_sums(b):
                pe.wait_ge(s_osum, (NK - 1) * (b.j + 1))
                if not first(b, NBLK - 1):
                    pe.wait_ge(s_t1lo, NT * (b.j + 2) - 1)
                for n in range(NT):
                    last = nc.tensor.matmul(tp[1][:, n:n + 1], osum[:, tok(n)], ones[:, :], start=True, stop=True)
                last.then_inc(s_rms, 1)

            def attention_out(b, n):
                if n == 0:
                    pe.wait_ge(s_oglo, NK * (b.j + 1))
                    if first(b, 0):
                        pe.wait_ge(s_wlo_pool, 2)
                if n < 3:
                    if not first(b, 0):
                        pe.wait_ge(s_ob, NT * (b.j - 1) + n + 2)
                else:
                    pe.wait_ge(s_x1, NT * b.j + 1)
                terms = [(ogT_h[:, k, tok(n)], ogT_l[:, k, tok(n)], wo_h[:, k, :], wo_l[:, k, :]) for k in range(NK)]
                product(main_c(n)[:, :], terms).then_inc(s_c, 1)

            def first_attention_out(b):
                pe.wait_ge(s_wlo_pool, 2)
                pe.wait_ge(s_oglo, NK - 1)
                def terms(n, ks):
                    return [(ogT_h[:, k, tok(n)], ogT_l[:, k, tok(n)], wo_h[:, k, :], wo_l[:, k, :]) for k in ks]
                for n in range(3):
                    product(main_c(n)[:, :], terms(n, range(NK - 1)), stop=False)
                rms_sums(b)
                pe.wait_ge(s_oglo, NK)
                for n in range(3):
                    product(main_c(n)[:, :], terms(n, [NK - 1]), start=False).then_inc(s_c, 1)
                attention_out(b, 3)

            pe.wait_ge(s_const, 2)
            for n in range(NT):
                transposes(Block(0, 0, 0), n, T1_FIRST[n], s_xn1, s_t1)

            def step(prev, now, nxt):
                for q in range(3):
                    projection(now, 0, q)
                if prev is not None:
                    norm2_transposes(prev, 0)
                    norm2_transposes(prev, 1)
                projection(now, 1, QF)
                if prev is not None:
                    norm2_transposes(prev, 2)
                projection(now, 1, QI)
                if prev is not None:
                    norm2_transposes(prev, 3)
                projection(now, 1, QG)
                if prev is not None:
                    for n in range(NT):
                        expert_first(prev, n)
                for q in range(3):
                    projection(now, 2, q)
                projection(now, 3, QF)
                projection(now, 3, QI)
                if prev is not None:
                    lora_transposes(prev)
                projection(now, 3, QG)
                for n in range(NT):
                    if prev is not None:
                        expert_second(prev, n)
                    if nxt is not None:
                        norm1_transposes(nxt, n)
                if prev is None:
                    first_attention_out(now)
                    return
                rms_sums(now)
                for n in range(NT):
                    attention_out(now, n)
                    if nxt is None and n > 1:
                        norm2_transposes(now, n - 2)

            flow(pe, step)
            expert_first(LAST, 0)
            norm2_transposes(LAST, 2)
            norm2_transposes(LAST, 3)
            expert_first(LAST, 1)
            expert_first(LAST, 2)
            expert_first(LAST, 3)
            dst = [main_e2(0), main_e2(1), bank[0], bank[1]]
            pe.wait_ge(s_x1w, NT * LAST.j + 3)
            for n in range(NT):
                terms = [(x2T_h[:, k, tok(n)], x2T_l[:, k, tok(n)], wffn_h[:, k, 0:HALF], wffn_l[:, k, 0:HALF])
                         for k in range(NK)]
                product(dst[n][:, 0:HALF], terms, stop=False)
                if n == 1:
                    lora_transposes(LAST)
            pe.wait_ge(s_hwlo, NBLK)
            for n in range(NT):
                for cols, start in ((slice(0, HALF), False), (slice(HALF, D), True)):
                    last = product(dst[n][:, cols], [(hwT_h[:, tok(n)], hwT_l[:, tok(n)], wb_h[:, cols], wb_l[:, cols])],
                                   start=start)
                last.then_inc(s_e2, 1)


def kernel(L0_attn_hidden_states, L0_attn_Wi, L0_attn_Wf, L0_attn_Wg, L0_attn_Wo, L0_attn_g_norm_weight,
           L0_ffn_W, L0_ffn_gate_w, L0_ffn_A, L0_ffn_B):
    import numpy as np
    import concourse.bacc as bacc
    from concourse.bass_utils import run_bass_kernel_spmd

    P = 128
    x = np.ascontiguousarray(L0_attn_hidden_states)
    D = x.shape[-1]
    NK = D // P
    E, R, _ = L0_ffn_A.shape
    wproj = np.stack([np.asarray(w).reshape(NK, P, NK, P) for w in (L0_attn_Wf, L0_attn_Wi, L0_attn_Wg)])
    wproj = wproj.transpose(3, 2, 0, 1, 4).reshape(NK, P, 3 * NK * P)
    wo = np.asarray(L0_attn_Wo).reshape(NK, P, D).transpose(1, 0, 2)
    wffn = np.concatenate([np.asarray(L0_ffn_W).T, np.asarray(L0_ffn_A).reshape(E * R, D).T, np.asarray(L0_ffn_gate_w).T], axis=1)
    wffn = wffn.reshape(NK, P, -1).transpose(1, 0, 2)
    wb = np.asarray(L0_ffn_B).transpose(0, 2, 1).reshape(E * R, D)
    gn = np.asarray(L0_attn_g_norm_weight).reshape(NK, P).T
    arrays = {"x": x, "gn": gn, "wproj": wproj, "wo": wo, "wffn": wffn, "wb": wb}
    arrays = {f"in_{name}": np.ascontiguousarray(a) for name, a in arrays.items()}

    nc = bacc.Bacc("TRN2", target_bir_lowering=False, num_devices=1)
    ins = [nc.dram_tensor(name, a.shape, mybir.dt.from_np(a.dtype), kind="ExternalInput").ap() for name, a in arrays.items()]
    out = nc.dram_tensor("out", x.shape, mybir.dt.from_np(x.dtype), kind="ExternalOutput").ap()
    hgrn_lora_moe(nc, *ins, out)
    return run_bass_kernel_spmd(nc, [arrays], core_ids=[0]).results[0]["out"]
```

```python
from collections import namedtuple
from contextlib import ExitStack

import concourse.bass as bass
from concourse import mybir

Block = namedtuple("Block", "j par tb")


def hgrn_lora_moe(nc, x_in, xT_in, gn_in, wproj_in, wo_in, wffn_in, wb_in, out):
    F32, F32R, U32 = mybir.dt.float32, mybir.dt.float32r, mybir.dt.uint32
    ALU, ACT = mybir.AluOpType, mybir.ActivationFunctionType

    P = 128
    NSEQ, SEQ, D = x_in.shape
    NT = 4
    TOK = NT * P
    NBLK = NSEQ * SEQ // TOK
    NK = D // P
    ER = wb_in.shape[0]
    FW = wffn_in.shape[2]
    E = FW - D - ER
    R = ER // E
    HALF = FW // 2
    REST = D - HALF
    EPS, ALPHA = 1e-5, 16.0
    PROJ = 3 * NK * P
    QF, QI, QG = range(3)
    SQ = 32
    NSQ = P // SQ
    MOVES = 2 * NSQ * NSQ

    x_v = x_in.rearrange("b (t n p) d -> b t p n d", n=NT, p=P)
    xT_v = xT_in.rearrange("b (k p) (t m) -> b t p k m", p=P, m=TOK)
    stats_row = nc.dram_tensor("stats_row", [2 * NT, P], F32).ap()

    ctx = ExitStack()
    with ctx:
        def sb(name, shape, dt=F32):
            return ctx.enter_context(nc.sbuf_tensor(name, shape, dt))

        def pb(name):
            return ctx.enter_context(nc.psum_tensor(name, [P, 512], F32))

        def sem(name):
            return ctx.enter_context(nc.semaphore(name))

        wproj_h = sb("wproj_h", [P, NK, 3, NK, P], F32R)
        wproj_l = sb("wproj_l", [P, NK, 3, NK, P], F32R)
        wo_h = sb("wo_h", [P, NK, D], F32R)
        wo_l = sb("wo_l", [P, NK, D], F32R)
        wffn_h = sb("wffn_h", [P, NK, FW], F32R)
        wffn_l = sb("wffn_l", [P, NK, FW], F32R)
        wb_h = sb("wb_h", [ER, D], F32R)
        wb_l = sb("wb_l", [ER, D], F32R)
        gn = sb("gn", [P, NK])
        x = [sb(f"x_seq{i}", [P, NT, D]) for i in range(2)]
        x1 = sb("x1", [P, NT, D])
        xn = sb("xn", [P, NT, D])
        outb = sb("outb", [P, 2, D])
        xT = sb("xT", [P, NK, TOK])
        stats_bc = sb("stats_bc", [P, NT, 2, P])
        xnT_h = sb("xnT_h", [P, NK, TOK], F32R)
        xnT_l = sb("xnT_l", [P, NK, TOK], F32R)
        x2T_h = sb("x2T_h", [P, NK, TOK], F32R)
        x2T_l = sb("x2T_l", [P, NK, TOK], F32R)
        ogT_h = sb("ogT_h", [P, NK, TOK], F32R)
        ogT_l = sb("ogT_l", [P, NK, TOK], F32R)
        decay = sb("decay", [P, TOK])
        inject = sb("inject", [P, TOK])
        value = sb("value", [P, TOK])
        gate = sb("gate", [P, TOK])
        o = sb("o", [P, TOK])
        osum = sb("osum", [P, TOK])
        osq_part = sb("osq_part", [P, NT * NSQ])
        carry = sb("carry", [P, NSEQ, NK])
        h = sb("h", [P, NT, ER + E])
        top = sb("top", [P, NT, 8])
        topi = sb("topi", [P, NT, 8], U32)
        gap = sb("gap", [P, NT])
        topw = sb("topw", [P, NT, 2])
        pick = sb("pick", [P, NT, 2, E])
        wmat = sb("wmat", [P, NT, E])
        hw = sb("hw", [P, NT, ER])
        hwT_h = sb("hwT_h", [ER, TOK], F32R)
        hwT_l = sb("hwT_l", [ER, TOK], F32R)
        bn1, ve1 = sb("bn1", [P, NT, 6]), sb("ve1", [P, NT])
        stats1, stats1T = sb("stats1", [P, SQ]), sb("stats1T", [P, SQ])
        mv1 = stats1[:, 0:2 * NT].rearrange("p (n s) -> p n s", s=2)
        bn2, mv2, ve2, rstd2 = (sb(n, s) for n, s in (("bn2", [P, NT, 6]), ("mv2", [P, NT, 2]), ("ve2", [P, NT]), ("rstd2", [P, NT])))
        ms, rr = sb("ms", [P, NT]), sb("rr", [P, NT])
        ident = sb("ident", [P, P])
        quads = sb("quads", [P, P])
        minus_half = sb("minus_half", [P, NT])
        expert_no = sb("expert_no", [P, E])

        bank = [pb(n) for n in ("psum_f", "psum_i", "psum_g")]
        tp = [pb("psum_t0"), pb("psum_t1")]
        main = [pb(f"psum_m{i}") for i in range(3)]

        def bank_e1(n):
            return tp[0] if n == NT - 1 else main[n]

        def bank_e2(n):
            return tp[0] if n == NT - 1 else main[(n + 1) % 3]

        def bank_wo(n):
            return tp[0] if n == NT - 1 else main[(n + 2) % 3]

        def is_block(b, j):
            return b is not None and isinstance(b.j, int) and b.j == j

        def transposed_by_pe(b):
            return is_block(b, 0) or is_block(b, NBLK - 1)

        def bank_t2(b, n):
            return tp[1] if n % 2 else tp[0] if is_block(b, 0) else bank[QG]

        T1_FIRST = [tp[1], tp[0], main[0], main[1]]

        def tile_of(featT, n):
            return featT[:, :, n * P:(n + 1) * P]

        def half_of(featT, i):
            return featT[:, :, i * TOK // 2:(i + 1) * TOK // 2]

        def by_chunk(psum):
            return psum[:, :].rearrange("p (k t) -> p k t", t=P)

        s_x = [sem("x_seq0_loaded"), sem("x_seq1_loaded")]
        s_xt = [sem(f"x_tile{n}_loaded") for n in range(NT)]
        s_gn = sem("gn_loaded")
        s_xT = sem("xT_loaded")
        s_row, s_bc = sem("stats_row_stored"), sem("stats_broadcast")
        s_out = [sem("out0_stored"), sem("out1_stored")]
        s_const = sem("constants_made")
        s_ident, s_quads = sem("ident_zeroed"), sem("quads_made")
        s_gnw = sem("wo_scaled")
        s_table = sem("sigmoid_table_loaded")
        s_whi, s_wlo, s_wlo_pool = sem("weights_hi"), sem("weights_lo"), sem("weights_lo_by_pool")
        s_proj = [sem("f_done"), sem("i_done"), sem("g_done")]
        s_t1, s_t2, s_hwt = sem("t1_done"), sem("t2_done"), sem("hwt_done")
        s_e1, s_e2, s_rms, s_c = sem("e1_done"), sem("e2_done"), sem("rms_done"), sem("c_done")
        s_decay, s_inject, s_value, s_gate = sem("decay_ready"), sem("inject_ready"), sem("value_ready"), sem("gate_ready")
        s_sq, s_oghi = sem("osq_ready"), sem("og_hi")
        s_t1hi, s_t2hi, s_hwhi = sem("t1_hi"), sem("t2_hi"), sem("hw_hi")
        s_h, s_topw = sem("h_copied"), sem("topw_ready")
        s_u, s_v, s_scan, s_carry = sem("silu_i"), sem("scan_input"), sem("scan_done"), sem("carry_saved")
        s_w, s_og, s_oglo, s_osum = sem("silu_g"), sem("og_ready"), sem("og_lo"), sem("osum_ready")
        s_oT, s_part = sem("osum_transposed"), sem("osq_part_ready")
        s_t1lo, s_t2lo, s_hwlo = sem("t1_lo"), sem("t2_lo"), sem("hw_lo")
        s_x1w, s_top, s_topi, s_gap = sem("x1_rest"), sem("top_ready"), sem("topi_ready"), sem("gap_ready")
        s_eq, s_pick, s_wmat, s_hw = sem("eq_ready"), sem("pick_ready"), sem("wmat_ready"), sem("hw_ready")
        s_ob, s_ms, s_x1 = sem("out_ready"), sem("ms_ready"), sem("x1_ready")
        s_bn1, s_mv1, s_ve1, s_xn1 = sem("bn1_done"), sem("mv1_done"), sem("ve1_ready"), sem("xn1_ready")
        s_st0, s_stT = sem("stats1_zeroed"), sem("stats_transposed")
        s_cen, s_xnT = sem("xT_centred"), sem("xnT_ready")
        s_x2sq, s_x2mv = sem("x2_squares_transposed"), sem("x2_squares_moved")
        s_bn2, s_mv2, s_ve2, s_xn2 = sem("bn2_done"), sem("mv2_done"), sem("ve2_ready"), sem("xn2_ready")
        s_zero = sem("carry_zeroed")
        s_rstd1, s_rr, s_rstd2 = sem("rstd1_ready"), sem("rr_ready"), sem("rstd2_ready")

        def flow(eng, step):
            b0, b1, b2 = Block(0, 0, 0), Block(1, 1, 0), Block(2, 0, 1)
            step(None, b0, b1)
            step(b0, b1, b2)
            with eng.Fori(1, NBLK // 2 - 1) as k:
                step(Block(2 * k - 1, 1, k - 1), Block(2 * k, 0, k), Block(2 * k + 1, 1, k))
                step(Block(2 * k, 0, k), Block(2 * k + 1, 1, k), Block(2 * k + 2, 0, k + 1))
            b5, b6, b7 = (Block(NBLK - i, (NBLK - i) % 2, (NBLK - i) // 2) for i in (3, 2, 1))
            step(b5, b6, b7)
            step(b6, b7, None)

        LAST = Block(NBLK - 1, 1, NBLK // 2 - 1)

        moved = [ap.rearrange("p (k t) -> p k t", k=NK) for ap in (
            stats_bc[:, :, :, :].rearrange("p n s t -> p (n s t)"), outb[:, :, :].rearrange("p n d -> p (n d)"))]

        def out_tile(b, n):
            return x1[:, n, :] if b is LAST else outb[:, n % 2, :]

        AREAS = [ap[:, :, :].rearrange("p n d -> p (n d)") for ap in (x1, x[1], xT, outb, xn)]
        GROUPS = []

        def flat(ap):
            return ap.rearrange("p k n -> p (k n)")

        def group(area, src, hi, lo, at=0):
            GROUPS.append((src, AREAS[area][:, at:at + src.shape[1]], hi, lo, area))

        QW = NK * P
        for q in range(3):
            group(0, wproj_in[0][:, q * QW:(q + 1) * QW], flat(wproj_h[:, 0, q]), flat(wproj_l[:, 0, q]), at=q * QW)
        for c, area in ((1, 1), (2, 2), (3, 0)):
            group(area, wproj_in[c], wproj_h[:, c].rearrange("p q k n -> p (q k n)"),
                  wproj_l[:, c].rearrange("p q k n -> p (q k n)"))
        G1, G2, G3, G_FFN0, G_WO, G_FFN1, G_B = range(3, 10)
        lo_half, hi_half = slice(0, NK // 2), slice(NK // 2, NK)
        group(4, flat(wffn_in[:, lo_half, :]), flat(wffn_h[:, lo_half, :]), flat(wffn_l[:, lo_half, :]))
        group(0, flat(wo_in), flat(wo_h[:, :, :]), flat(wo_l[:, :, :]))
        group(4, flat(wffn_in[:, hi_half, :]), flat(wffn_h[:, hi_half, :]), flat(wffn_l[:, hi_half, :]))
        group(3, wb_in, wb_h[:, :], wb_l[:, :])
        AFTER = {G3: 2, G_WO: G3}
        s_stage = [sem(f"weights{g}_loaded") for g in range(len(GROUPS))]
        BY_POOL = (0, G_FFN0, G_WO, G_FFN1, G_B)

        block = ctx.enter_context(nc.Block())

        @block.sync
        def _(sp):
            def load_x(b):
                sp.dma_start(x[b.par][:, :, :], x_v[b.par, b.tb]).then_inc(s_x[b.par], 16)

            def load_xT(b):
                sp.dma_start(xT[:, :, :], xT_v[b.par, b.tb]).then_inc(s_xT, 16)

            def broadcast_stats(b):
                sp.wait_ge(s_stT, b.j)
                for q in range(NSQ):
                    sp.dma_start(stats_row[:, q * SQ:(q + 1) * SQ], stats1T[q * SQ:q * SQ + 2 * NT, :]).then_inc(s_row, 16)
                sp.wait_ge(s_row, NSQ * 16 * b.j)
                sp.dma_start(stats_bc[:, :, :, :].rearrange("p n s t -> p (n s t)"),
                             stats_row.rearrange("c t -> (c t)").partition_broadcast(P)).then_inc(s_bc, 16)

            def store_out(b):
                for n in range(NT):
                    sp.wait_ge(s_ob, NT * b.j + n + 1)
                    sp.dma_start(out[b.par, bass.ds(b.tb * TOK + n * P, P), :], out_tile(b, n)).then_inc(s_out[n % 2], 16)

            def load_x_tile(n):
                sp.dma_start(x[0][:, n, :], x_v[0, 0][:, n, :]).then_inc(s_xt[n], 16)

            def load_group(g):
                if g in AFTER:
                    sp.wait_ge(s_wlo, AFTER[g])
                sp.dma_start(GROUPS[g][1], GROUPS[g][0]).then_inc(s_stage[g], 16)

            load_x_tile(0)
            load_x_tile(1)
            load_group(0)
            load_x_tile(2)
            load_x_tile(3)
            for g in (1, 2, G1, G2):
                load_group(g)
            sp.dma_start(gn[:, :], gn_in).then_inc(s_gn, 16)
            load_group(G_B)
            load_group(G3)
            sp.wait_ge(s_t1, NT)
            load_group(G_FFN0)
            sp.wait_ge(s_wlo, G1)
            load_x(Block(1, 1, 0))
            sp.wait_ge(s_wlo, G2)
            load_xT(Block(1, 1, 0))
            load_group(G_WO)
            sp.wait_ge(s_wlo_pool, 2)
            load_group(G_FFN1)

            def step(prev, now, nxt):
                if prev is not None and nxt is not None:
                    sp.wait_ge(s_x1, NT * now.j)
                    load_x(nxt)
                    sp.wait_ge(s_t1lo, NK * now.j + NK)
                    load_xT(nxt)
                if nxt is not None:
                    broadcast_stats(nxt)
                if prev is not None:
                    store_out(prev)

            flow(sp, step)
            store_out(LAST)
            for i in range(2):
                sp.wait_ge(s_out[i], NBLK * NT // 2 * 16)

        @block.gpsimd
        def _(pool):
            nc.gpsimd.memset(ident[:, :], 0.0).then_inc(s_ident, 1)
            pool.wait_ge(s_ident, 1)
            nc.gpsimd.affine_select(out=ident[:, :], in_=ident[:, :], compare_op=ALU.not_equal, fill=1.0,
                                    base=0, pattern=[[-1, P]], channel_multiplier=1).then_inc(s_const, 1)
            nc.gpsimd.memset(minus_half[:, :], -0.5).then_inc(s_const, 1)
            for e in range(E):
                nc.gpsimd.memset(expert_no[:, e:e + 1], float(e)).then_inc(s_const, 1)
            pool.wait_ge(s_const, 2)

            def norm1(b):
                pool.wait_ge(s_ve1, 2 * b.j + NT)
                nc.gpsimd.tensor_tensor(mv1[:, :, 1], ve1[:, :], minus_half[:, :], ALU.pow).then_inc(s_rstd1, 1)

            def centre(b):
                pool.wait_ge(s_bc, 16 * b.j)
                pool.wait_ge(s_xT, 16 * b.j)
                for k in range(NK):
                    part = xT[:, k, :].rearrange("p (n t) -> p n t", t=P)
                    nc.gpsimd.tensor_tensor(part, part, stats_bc[:, :, 0, :], ALU.subtract).then_inc(s_cen, 1)

            def split_weights(g):
                _, raw, hi, lo, _ = GROUPS[g]
                if g == G_WO:
                    pool.wait_ge(s_stage[g], 16)
                    pool.wait_ge(s_gn, 16)
                    for k in range(NK):
                        part = raw[:, k * D:(k + 1) * D]
                        nc.gpsimd.tensor_scalar(part, part, gn[:, k:k + 1], 1.0, ALU.mult, ALU.mult).then_inc(s_gnw, 1)
                    pool.wait_ge(s_gnw, NK)
                pool.wait_ge(s_whi, g + 1)
                nc.gpsimd.tensor_tensor(lo, raw, hi.bitcast(F32), ALU.subtract).then_inc(s_wlo_pool, 1)

            for n in range(NT):
                pool.wait_ge(s_ve1, n + 1)
                nc.gpsimd.tensor_tensor(mv1[:, n, 1:2], ve1[:, n:n + 1], minus_half[:, 0:1],
                                        ALU.pow).then_inc(s_rstd1, 1)
                if n == 1:
                    split_weights(0)

            split_weights(G_FFN0)
            split_weights(G_WO)

            def step(prev, now, nxt):
                if nxt is not None:
                    norm1(nxt)
                if prev is None:
                    split_weights(G_FFN1)
                    split_weights(G_B)
                if nxt is not None:
                    centre(nxt)
                pool.wait_ge(s_ms, NSQ * (now.j + 1))
                nc.gpsimd.tensor_tensor(rr[:, :], ms[:, :], minus_half[:, :], ALU.pow).then_inc(s_rr, 1)
                for n in range(NT):
                    pool.wait_ge(s_ve2, NT * now.j + n + 1)
                    nc.gpsimd.tensor_tensor(rstd2[:, n:n + 1], ve2[:, n:n + 1], minus_half[:, 0:1],
                                            ALU.pow).then_inc(s_rstd2, 1)

            flow(pool, step)

        @block.scalar
        def _(act):
            def split_weights(g):
                _, raw, hi, _, _ = GROUPS[g]
                if g == G_WO:
                    act.wait_ge(s_gnw, NK)
                else:
                    act.wait_ge(s_stage[g], 16)
                nc.scalar.activation(hi, raw, ACT.Copy).then_inc(s_whi, 1)

            def first_t1_hi(n):
                act.wait_ge(s_t1, n + 1)
                nc.scalar.activation(tile_of(xnT_h, n), by_chunk(T1_FIRST[n]), ACT.Copy).then_inc(s_t1hi, 1)

            def t1_hi(now, b, k):
                if k == 0:
                    act.wait_ge(s_proj[QG], NK * now.j + NK)
                act.wait_ge(s_xnT, NK * (b.j - 1) + k + 1)
                nc.scalar.activation(xnT_h[:, k, :], xT[:, k, :], ACT.Copy).then_inc(s_t1hi, 1)

            def x2_moves(b, i, groups):
                act.wait_ge(s_x2sq, NT * (b.j - 1) + (i + 1) * NT // 2)
                for q in groups:
                    for r in range(NSQ):
                        src = xn[q * SQ:(q + 1) * SQ, i * NT // 2:(i + 1) * NT // 2, :].rearrange(
                            "p n (k r t) -> p k r n t", r=NSQ, t=SQ)[:, :, r]
                        dst = moved[i][r * SQ:(r + 1) * SQ].rearrange(
                            "p k (n q t) -> p k n q t", q=NSQ, t=SQ)[:, :, :, q]
                        nc.scalar.activation(dst, src, ACT.Copy).then_inc(s_x2mv, 1)

            def x2_hi(b, i):
                act.wait_ge(s_x2mv, MOVES * (b.j - 1) + (i + 1) * MOVES // 2)
                nc.scalar.activation(half_of(x2T_h, i), moved[i], ACT.Copy).then_inc(s_t2hi, NT // 2)

            def t2_hi(b, n):
                act.wait_ge(s_t2, n + 1 + (0 if is_block(b, 0) else NT))
                nc.scalar.activation(tile_of(x2T_h, n), by_chunk(bank_t2(b, n)), ACT.Copy).then_inc(s_t2hi, 1)

            def forget(b, c):
                act.wait_ge(s_proj[QF], NK * b.j + c + 1)
                if not (is_block(b, 0) and c == 0):
                    act.wait_ge(s_scan, NK * b.j + c)
                if c > 1:
                    act.wait_ge(s_osum, (NK - 1) * b.j + c - 1)
                elif c == 0 and not is_block(b, 0):
                    act.wait_ge(s_part, b.j)
                nc.scalar.activation(decay[:, :], bank[QF][:, :], ACT.Sigmoid).then_inc(s_decay, 1)
                nc.scalar.activation(inject[:, :], bank[QF][:, :], ACT.Sigmoid, scale=-1.0).then_inc(s_inject, 1)

            def put(b, c):
                act.wait_ge(s_proj[QI], NK * b.j + c + 1)
                nc.scalar.activation(value[:, :], bank[QI][:, :], ACT.Sigmoid).then_inc(s_value, 1)

            def output_gate(b, c):
                act.wait_ge(s_proj[QG], NK * b.j + c + 1)
                if not (is_block(b, 0) and c == 0):
                    act.wait_ge(s_oglo, NK * b.j + c)
                nc.scalar.activation(gate[:, :], bank[QG][:, :], ACT.Sigmoid).then_inc(s_gate, 1)

            def square(b, c):
                act.wait_ge(s_scan, NK * b.j + c + 1)
                if c == 0:
                    if not is_block(b, 0):
                        act.wait_ge(s_oT, b.j)
                    dst = osum
                else:
                    dst = inject
                nc.scalar.activation(dst[:, :], o[:, :], ACT.Square).then_inc(s_sq, 1)

            def og_hi(b, c):
                act.wait_ge(s_og, NK * b.j + c + 1)
                if c == 0 and not is_block(b, 0):
                    act.wait_ge(s_c, NT * b.j)
                nc.scalar.activation(ogT_h[:, c, :], gate[:, :], ACT.Copy).then_inc(s_oghi, 1)

            def expert_inputs(b):
                if b is LAST:
                    t2_hi(b, 0)
                    t2_hi(b, 1)
                for n in range(NT):
                    if b is LAST and n + 2 < NT:
                        t2_hi(b, n + 2)
                    act.wait_ge(s_e1, NT * b.j + n + 1)
                    nc.scalar.activation(h[:, n, :], bank_e1(n)[:, REST:HALF], ACT.Copy).then_inc(s_h, 1)
                act.wait_ge(s_gap, b.j + 1)
                nc.scalar.activation(topw[:, :, 0], gap[:, :], ACT.Sigmoid).then_inc(s_topw, 1)
                nc.scalar.activation(topw[:, :, 1], gap[:, :], ACT.Sigmoid, scale=-1.0).then_inc(s_topw, 1)

            def hw_hi(b):
                act.wait_ge(s_hwt, b.j + 1)
                nc.scalar.activation(hwT_h[:, :], tp[0][:, :], ACT.Copy).then_inc(s_hwhi, 1)

            act.wait_ge(s_const, 2)
            nc.scalar.activation(topw[:, :, 0], minus_half[:, :], ACT.Sigmoid).then_inc(s_table, 1)
            for n in range(NT):
                if n < 3:
                    split_weights(n)
                first_t1_hi(n)

            def step(prev, now, nxt):
                if prev is None:
                    split_weights(G1)
                    split_weights(G2)
                moves = prev is not None and not transposed_by_pe(prev)
                for c in range(NK):
                    forget(now, c)
                    if prev is None and c > 0:
                        split_weights((G_FFN0, G_WO, G_FFN1)[c - 1])
                    if moves and c < 2:
                        x2_moves(prev, c, (0, 1))
                    put(now, c)
                    if moves and c == 0:
                        x2_moves(prev, c, (2, 3))
                    if prev is None and c == 0:
                        split_weights(G3)
                    if prev is None and c == 3:
                        split_weights(G_B)
                    output_gate(now, c)
                    if prev is not None and c == 3:
                        hw_hi(prev)
                    if moves and c == 1:
                        x2_moves(prev, c, (2, 3))
                    if is_block(prev, 0) and c == 1:
                        t2_hi(prev, 2)
                        t2_hi(prev, 3)
                    square(now, c)
                    if is_block(prev, 0) and c == 0:
                        t2_hi(prev, 0)
                        t2_hi(prev, 1)
                    og_hi(now, c)
                    if moves and c < 2:
                        x2_hi(prev, c)
                    if prev is not None and c == 2:
                        expert_inputs(prev)
                if nxt is not None:
                    for k in range(NK):
                        t1_hi(now, nxt, k)
                if prev is not None:
                    act.wait_ge(s_hw, prev.j + 1)

            flow(act, step)
            expert_inputs(LAST)
            hw_hi(LAST)

        @block.vector
        def _(dve):
            def split_weights(g):
                _, raw, hi, lo, _ = GROUPS[g]
                dve.wait_ge(s_whi, g + 1)
                nc.vector.tensor_tensor(lo, raw, hi.bitcast(F32), ALU.subtract).then_inc(s_wlo, 1)

            def norm1_stats(b):
                dve.wait_ge(s_x[b.par], 16 * (b.tb + b.par))
                for n in range(NT):
                    if n > 0:
                        dve.wait_ge(s_bn1, NT * b.j + n)
                    nc.vector.bn_stats(bn1[:, n, :], x[b.par][:, n, :]).then_inc(s_bn1, 1)
                    if n > 0:
                        nc.vector.bn_aggr(mv1[:, n - 1, :], bn1[:, n - 1, :]).then_inc(s_mv1, 1)
                dve.wait_ge(s_mv1, NT * b.j + NT - 1)
                dve.wait_ge(s_bn1, NT * b.j + NT)
                nc.vector.tensor_scalar(ve1[:, 0:NT - 1], mv1[:, 0:NT - 1, 1], EPS, None, ALU.add).then_inc(s_ve1, 1)
                nc.vector.bn_aggr(mv1[:, NT - 1, :], bn1[:, NT - 1, :]).then_inc(s_mv1, 1)
                dve.wait_ge(s_mv1, NT * b.j + NT)
                nc.vector.tensor_scalar(ve1[:, NT - 1:NT], mv1[:, NT - 1, 1:2], EPS, None, ALU.add).then_inc(s_ve1, 1)

            def norm1_send(b):
                dve.wait_ge(s_rstd1, b.j + NT)
                nc.vector.transpose(stats1T[:, :], stats1[:, :]).then_inc(s_stT, 1)

            def norm1_apply(b, k):
                dve.wait_ge(s_cen, NK * (b.j - 1) + k + 1)
                part = xT[:, k, :].rearrange("p (n t) -> p n t", t=P)
                nc.vector.tensor_tensor(part, part, stats_bc[:, :, 1, :], ALU.mult).then_inc(s_xnT, 1)

            def first_t1_lo(n):
                dve.wait_ge(s_t1hi, n + 1)
                nc.vector.tensor_tensor(tile_of(xnT_l, n), by_chunk(T1_FIRST[n]), tile_of(xnT_h, n).bitcast(F32),
                                        ALU.subtract).then_inc(s_t1lo, 1)

            def t1_lo(b, k):
                dve.wait_ge(s_t1hi, NK * b.j + k + 1)
                nc.vector.tensor_tensor(xnT_l[:, k, :], xT[:, k, :], xnT_h[:, k, :].bitcast(F32),
                                        ALU.subtract).then_inc(s_t1lo, 1)

            def x2_lo(b, i):
                dve.wait_ge(s_t2hi, NT * b.j + (i + 1) * NT // 2)
                nc.vector.tensor_tensor(half_of(x2T_l, i), moved[i], half_of(x2T_h, i).bitcast(F32),
                                        ALU.subtract).then_inc(s_t2lo, NT // 2)

            def t2_lo(b, n):
                dve.wait_ge(s_t2hi, NT * b.j + n + 1)
                nc.vector.tensor_tensor(tile_of(x2T_l, n), by_chunk(bank_t2(b, n)), tile_of(x2T_h, n).bitcast(F32),
                                        ALU.subtract).then_inc(s_t2lo, 1)

            def silu_i(b, c):
                dve.wait_ge(s_value, NK * b.j + c + 1)
                nc.vector.tensor_tensor(value[:, :], bank[QI][:, :], value[:, :], ALU.mult).then_inc(s_u, 1)

            def scan(b, c):
                dve.wait_ge(s_u, NK * b.j + c + 1)
                dve.wait_ge(s_inject, NK * b.j + c + 1)
                nc.vector.tensor_tensor(value[:, :], value[:, :], inject[:, :], ALU.mult).then_inc(s_v, 1)
                dve.wait_ge(s_v, NK * b.j + c + 1)
                if not (is_block(b, 0) and c == 0):
                    dve.wait_ge(s_sq, NK * b.j + c)
                state = carry[:, b.par, c:c + 1]
                nc.vector.tensor_tensor_scan(o[:, :], decay[:, :], value[:, :], state,
                                             ALU.mult, ALU.add).then_inc(s_scan, 1)
                dve.wait_ge(s_scan, NK * b.j + c + 1)
                nc.vector.tensor_copy(state, o[:, TOK - 1:TOK]).then_inc(s_carry, 1)

            def gated(b, c):
                dve.wait_ge(s_gate, NK * b.j + c + 1)
                nc.vector.tensor_tensor(gate[:, :], bank[QG][:, :], gate[:, :], ALU.mult).then_inc(s_w, 1)
                dve.wait_ge(s_w, NK * b.j + c + 1)
                nc.vector.tensor_tensor(gate[:, :], o[:, :], gate[:, :], ALU.mult).then_inc(s_og, 1)
                if c > 0:
                    dve.wait_ge(s_sq, NK * b.j + c + 1)
                    if c > 1:
                        dve.wait_ge(s_osum, (NK - 1) * b.j + c - 1)
                    nc.vector.tensor_tensor(osum[:, :], osum[:, :], inject[:, :], ALU.add).then_inc(s_osum, 1)

            def og_lo(b, c):
                dve.wait_ge(s_oghi, NK * b.j + c + 1)
                nc.vector.tensor_tensor(ogT_l[:, c, :], gate[:, :], ogT_h[:, c, :].bitcast(F32),
                                        ALU.subtract).then_inc(s_oglo, 1)

            def expert_inputs(b):
                for n in range(NT):
                    if b is LAST and n + 2 < NT:
                        t2_lo(b, n + 2)
                    dve.wait_ge(s_h, NT * b.j + n + 1)
                    rest = x1[:, n, HALF:D]
                    nc.vector.tensor_tensor(rest, bank_e1(n)[:, 0:REST], rest, ALU.add).then_inc(s_x1w, 1)
                    logits = h[:, n, ER:ER + E]
                    nc.vector.max(top[:, n, :], logits).then_inc(s_top, 1)
                    dve.wait_ge(s_zero, 1)
                    dve.wait_ge(s_top, NT * b.j + n + 1)
                    nc.vector.max_index(topi[:, n, :], top[:, n, :], logits).then_inc(s_topi, 1)
                nc.vector.tensor_tensor(gap[:, :], top[:, :, 0], top[:, :, 1], ALU.subtract).then_inc(s_gap, 1)
                dve.wait_ge(s_topi, NT * b.j + NT)
                nc.vector.tensor_tensor(pick[:, :, :, :],
                                        expert_no[:, :].unsqueeze(1).unsqueeze(1).broadcast_to([P, NT, 2, E]),
                                        topi[:, :, 0:2].unsqueeze(3).broadcast_to([P, NT, 2, E]),
                                        ALU.is_equal).then_inc(s_eq, 1)
                dve.wait_ge(s_eq, b.j + 1)
                dve.wait_ge(s_topw, 2 * b.j + 2)
                flat_pick = pick[:, :, :, :].rearrange("p n s e -> p (n s) e")
                nc.vector.scalar_tensor_tensor(flat_pick, flat_pick, ALPHA,
                                               topw[:, :, :].rearrange("p n s -> p (n s)").unsqueeze(2).broadcast_to([P, NT * 2, E]),
                                               ALU.mult, ALU.mult).then_inc(s_pick, 1)
                dve.wait_ge(s_pick, b.j + 1)
                nc.vector.tensor_tensor(wmat[:, :, :], pick[:, :, 0, :], pick[:, :, 1, :], ALU.add).then_inc(s_wmat, 1)
                dve.wait_ge(s_wmat, b.j + 1)
                nc.vector.tensor_tensor(hw[:, :, :].rearrange("p n (e r) -> p n e r", r=R),
                                        h[:, :, 0:ER].rearrange("p n (e r) -> p n e r", r=R),
                                        wmat[:, :, :].unsqueeze(3).broadcast_to([P, NT, E, R]),
                                        ALU.mult).then_inc(s_hw, 1)

            def hw_lo(b):
                dve.wait_ge(s_hwhi, b.j + 1)
                nc.vector.tensor_tensor(hwT_l[:, :], tp[0][:, :], hwT_h[:, :].bitcast(F32),
                                        ALU.subtract).then_inc(s_hwlo, 1)

            def final(b, n, src):
                dve.wait_ge(s_e2, NT * b.j + n + 1)
                if n >= 2 and b is not LAST:
                    dve.wait_ge(s_out[n % 2], b.j * (NT // 2 * 16) + 16)
                if n == 0:
                    dve.wait_ge(s_x1w, NT * b.j + NT)
                nc.vector.tensor_tensor(out_tile(b, n), src[:, :], x1[:, n, :],
                                        ALU.add).then_inc(s_ob, 1)

            def squares_transposed(b):
                dve.wait_ge(s_osum, (NK - 1) * (b.j + 1))
                nc.vector.transpose(inject[:, :], osum[:, :]).then_inc(s_oT, 1)

            def partial_sums(b):
                dve.wait_ge(s_oT, b.j + 1)
                nc.vector.tensor_reduce(osq_part[:, :], inject[:, :].rearrange("p (b j) -> p b j", j=SQ),
                                        mybir.AxisListType.X, ALU.add).then_inc(s_part, 1)

            def mean_square(b):
                dve.wait_ge(s_rms, b.j + 1)
                for q in range(NSQ):
                    rows = slice(q * SQ, (q + 1) * SQ)
                    sums = tp[1][rows, 0:NT * NSQ].rearrange("p (n s) -> p n s", s=NSQ)
                    nc.vector.tensor_scalar(ms[rows, :], sums[:, :, q], 1.0 / D, EPS, ALU.mult, ALU.add).then_inc(s_ms, 1)

            def residual(b, n):
                dve.wait_ge(s_c, NT * b.j + n + 1)
                if n == 0:
                    dve.wait_ge(s_rr, b.j + 1)
                nc.vector.scalar_tensor_tensor(x1[:, n, :], bank_wo(n)[:, :], rr[:, n:n + 1], x[b.par][:, n, :],
                                               ALU.mult, ALU.add).then_inc(s_x1, 1)
                dve.wait_ge(s_x1, NT * b.j + n + 1)
                nc.vector.bn_stats(bn2[:, n, :], x1[:, n, :]).then_inc(s_bn2, 1)
                dve.wait_ge(s_zero, 1)
                dve.wait_ge(s_bn2, NT * b.j + n + 1)
                nc.vector.bn_aggr(mv2[:, n, :], bn2[:, n, :]).then_inc(s_mv2, 1)
                dve.wait_ge(s_mv2, NT * b.j + n + 1)
                nc.vector.tensor_scalar(ve2[:, n:n + 1], mv2[:, n, 1:2], EPS, None, ALU.add).then_inc(s_ve2, 1)

            def norm2_apply(b, n):
                by_pe = transposed_by_pe(b)
                if n == 0:
                    if is_block(b, 0):
                        dve.wait_ge(s_wlo_pool, len(BY_POOL))
                    elif is_block(b, 1):
                        dve.wait_ge(s_t2, NT)
                    else:
                        dve.wait_ge(s_x2mv, MOVES * (b.j - 1))
                    if not by_pe:
                        dve.wait_ge(s_sq, NK * b.j + NK)
                elif not by_pe:
                    dve.wait_ge(s_x2sq, NT * (b.j - 1) + n)
                dve.wait_ge(s_rstd2, NT * b.j + n + 1)
                dst = xn[:, n, :] if by_pe else o[:, :]
                nc.vector.tensor_scalar(dst, x1[:, n, :], mv2[:, n, 0:1], rstd2[:, n:n + 1],
                                        ALU.subtract, ALU.mult).then_inc(s_xn2, 1)
                if not by_pe:
                    dve.wait_ge(s_xn2, NT * b.j + n + 1)
                    nc.vector.transpose(xn[:, n, :], o[:, :]).then_inc(s_x2sq, 1)

            nc.vector.memset(stats1[:, :], 0.0).then_inc(s_st0, 1)
            nc.vector.memset(carry[:, :, :], 0.0).then_inc(s_zero, 1)
            dve.wait_ge(s_st0, 1)
            dve.wait_ge(s_const, 1)
            for q in range(NSQ):
                rows = slice(q * SQ, (q + 1) * SQ)
                nc.vector.tensor_copy(quads[rows, :].rearrange("p (s i) -> p s i", i=SQ),
                                      ident[rows, rows].unsqueeze(1).broadcast_to([SQ, NSQ, SQ])).then_inc(s_quads, 1)

            def first_norm_stats(n):
                dve.wait_ge(s_xt[n], 16)
                nc.vector.bn_stats(bn1[:, n, :], x[0][:, n, :]).then_inc(s_bn1, 1)
                dve.wait_ge(s_bn1, n + 1)
                nc.vector.bn_aggr(mv1[:, n, :], bn1[:, n, :]).then_inc(s_mv1, 1)
                dve.wait_ge(s_mv1, n + 1)
                nc.vector.tensor_scalar(ve1[:, n:n + 1], mv1[:, n, 1:2], EPS, None, ALU.add).then_inc(s_ve1, 1)

            def first_norm_apply(n):
                dve.wait_ge(s_rstd1, n + 1)
                nc.vector.tensor_scalar(xn[:, n, :], x[0][:, n, :], mv1[:, n, 0:1], mv1[:, n, 1:2],
                                        ALU.subtract, ALU.mult).then_inc(s_xn1, 1)

            first_norm_stats(0)
            for n in range(1, NT):
                first_norm_stats(n)
                first_norm_apply(n - 1)
            first_t1_lo(0)
            first_norm_apply(NT - 1)
            for n in range(1, NT):
                first_t1_lo(n)
            split_weights(1)
            split_weights(2)
            dve.wait_ge(s_zero, 1)
            dve.wait_ge(s_const, 2 + E)

            def step(prev, now, nxt):
                if prev is None:
                    split_weights(G1)
                    split_weights(G2)
                for c in range(NK):
                    silu_i(now, c)
                    if c == 2 and prev is not None and nxt is not None:
                        norm1_send(nxt)
                    scan(now, c)
                    if prev is not None and c == 3:
                        hw_lo(prev)
                    if is_block(prev, 0) and c == 1:
                        t2_lo(prev, 2)
                        t2_lo(prev, 3)
                    if prev is None and c == 0:
                        split_weights(G3)
                    gated(now, c)
                    if is_block(prev, 0) and c == 0:
                        t2_lo(prev, 0)
                        t2_lo(prev, 1)
                    og_lo(now, c)
                    if prev is not None and not transposed_by_pe(prev) and c < 2:
                        x2_lo(prev, c)
                    if c == 1 and nxt is not None:
                        norm1_stats(nxt)
                    if c == 2 and prev is not None:
                        expert_inputs(prev)
                    if c == 2 and prev is None:
                        norm1_send(nxt)
                squares_transposed(now)
                if prev is not None:
                    partial_sums(now)
                for n in range(NT):
                    if nxt is not None:
                        norm1_apply(nxt, n)
                    if prev is None and n == 0:
                        partial_sums(now)
                    if prev is not None:
                        final(prev, n, bank_e2(n))
                    if nxt is not None and n > 0:
                        t1_lo(nxt, n - 1)
                    if n == 2:
                        mean_square(now)
                if nxt is not None:
                    t1_lo(nxt, NK - 1)
                residual(now, 0)
                for n in range(1, NT):
                    residual(now, n)
                    norm2_apply(now, n - 1)
                    if nxt is None and n > 1:
                        t2_lo(now, n - 2)
                if prev is not None:
                    for i in range(2):
                        dve.wait_ge(s_out[i], (prev.j + 1) * (NT // 2 * 16))
                norm2_apply(now, NT - 1)
                if prev is not None:
                    dve.wait_ge(s_hwt, prev.j + 1)

            flow(dve, step)
            expert_inputs(LAST)
            hw_lo(LAST)
            for n, src in enumerate((bank_e2(0), bank_e2(1), bank[0], bank[1])):
                final(LAST, n, src)

        @block.tensor
        def _(pe):
            def product(dst, terms, start=True, stop=True):
                for t, (lh, ll, rh, rl) in enumerate(terms):
                    nc.tensor.matmul(dst, lh, rh, start=start and t == 0, stop=False)
                    nc.tensor.matmul(dst, lh, rl, start=False, stop=False)
                    last = nc.tensor.matmul(dst, ll, rh, start=False, stop=stop and t == len(terms) - 1)
                return last

            def tok(n):
                return slice(n * P, (n + 1) * P)

            def transposes(b, n, dst, sem_xn, sem_done):
                pe.wait_ge(sem_xn, NT * b.j + n + 1)
                for k in range(NK):
                    last = nc.tensor.transpose(dst[:, k * P:(k + 1) * P], xn[:, n, k * P:(k + 1) * P], ident[:, :])
                last.then_inc(sem_done, 1)

            def norm2_transposes(b, n):
                if n == 0 and is_block(b, 0):
                    pe.wait_ge(s_x1, NT)
                elif n == 1:
                    pe.wait_ge(s_ms, NSQ * (b.j + 1))
                elif n > 1:
                    pe.wait_ge(s_t2lo, NT * b.j + n - 1)
                transposes(b, n, bank_t2(b, n), s_xn2, s_t2)

            def projection(b, c, q, half=None):
                cols = slice(0, TOK) if half is None else slice(half * TOK // 2, (half + 1) * TOK // 2)
                free = (s_inject, s_u, s_w)[q]
                if not (is_block(b, 0) and c == 0):
                    pe.wait_ge(free, NK * b.j + c)
                if is_block(b, 0) and (q == QF or c == 0):
                    if (c, q) == (0, QF):
                        pe.wait_ge(s_wlo_pool, 1)
                    else:
                        pe.wait_ge(s_wlo, q if c == 0 else (G1, G2, G3)[c - 1])
                if c == 0 and q == QF and is_block(b, 0):
                    pe.wait_ge(s_t1lo, NT // 2 if half == 0 else NT)
                for k in range(NK):
                    if c == 0 and q == QF and not is_block(b, 0):
                        pe.wait_ge(s_t1lo, NK * b.j + k + 1)
                    last = product(bank[q][:, cols], [(wproj_h[:, c, q, k, :], wproj_l[:, c, q, k, :],
                                                       xnT_h[:, k, cols], xnT_l[:, k, cols])],
                                   start=k == 0, stop=k == NK - 1)
                if half != 0:
                    last.then_inc(s_proj[q], 1)

            def expert_first(b, n):
                pe.wait_ge(s_t2lo, NT * b.j + n + 1)
                if n < 3:
                    pe.wait_ge(s_x1, NT * b.j + n + 2)
                if n == 0 and is_block(b, 0):
                    pe.wait_ge(s_wlo_pool, len(BY_POOL))
                terms = [(x2T_h[:, k, tok(n)], x2T_l[:, k, tok(n)], wffn_h[:, k, HALF:FW], wffn_l[:, k, HALF:FW])
                         for k in range(NK)]
                product(bank_e1(n)[:, 0:HALF], terms).then_inc(s_e1, 1)

            def lora_transposes(b):
                pe.wait_ge(s_hw, b.j + 1)
                for n in range(NT):
                    last = nc.tensor.transpose(tp[0][0:ER, tok(n)], hw[:, n, :], ident[:, :])
                last.then_inc(s_hwt, 1)

            def w_half(dst, n, start):
                terms = [(x2T_h[:, k, tok(n)], x2T_l[:, k, tok(n)], wffn_h[:, k, 0:HALF], wffn_l[:, k, 0:HALF])
                         for k in range(NK)]
                return product(dst[:, 0:HALF], terms, start=start, stop=not start)

            def lora(dst, n, cols, start, stop):
                return product(dst[:, cols], [(hwT_h[:, tok(n)], hwT_l[:, tok(n)], wb_h[:, cols], wb_l[:, cols])],
                               start=start, stop=stop)

            def w_then_lora(dst, n):
                lora(dst, n, slice(0, HALF), False, True)
                lora(dst, n, slice(HALF, D), True, True).then_inc(s_e2, 1)

            def expert_second(b):
                for n in range(2):
                    pe.wait_ge(s_x1w, NT * b.j + n + 2)
                    w_half(bank_e2(n), n, True)
                pe.wait_ge(s_hwlo, b.j + 1)
                for n in range(2):
                    w_then_lora(bank_e2(n), n)
                for n in range(2, NT):
                    lora(bank_e2(n), n, slice(0, D), True, False)
                    w_half(bank_e2(n), n, False).then_inc(s_e2, 1)

            def rms_sums(b):
                pe.wait_ge(s_part, b.j + 1)
                if is_block(b, 0):
                    pe.wait_ge(s_quads, NSQ)
                else:
                    pe.wait_ge(s_ms, NSQ * b.j)
                nc.tensor.matmul(tp[1][:, 0:NT * NSQ], quads[:, :], osq_part[:, :], start=True,
                                 stop=True).then_inc(s_rms, 1)

            def attention_out(b, n):
                if n == 0:
                    pe.wait_ge(s_oglo, NK * (b.j + 1))
                pe.wait_ge(s_ob, NT * (b.j - 1) + (2, 3, 3, 4)[n])
                terms = [(ogT_h[:, k, tok(n)], ogT_l[:, k, tok(n)], wo_h[:, k, :], wo_l[:, k, :]) for k in range(NK)]
                product(bank_wo(n)[:, :], terms).then_inc(s_c, 1)

            def first_attention_out(b):
                def terms(n, ks):
                    return [(ogT_h[:, k, tok(n)], ogT_l[:, k, tok(n)], wo_h[:, k, :], wo_l[:, k, :]) for k in ks]
                pe.wait_ge(s_wlo_pool, 3)
                pe.wait_ge(s_oglo, NK - 1)
                for n in range(NT):
                    product(bank_wo(n)[:, :], terms(n, range(NK - 1)), stop=False)
                rms_sums(b)
                pe.wait_ge(s_oglo, NK)
                for n in range(NT):
                    product(bank_wo(n)[:, :], terms(n, [NK - 1]), start=False).then_inc(s_c, 1)

            pe.wait_ge(s_const, 1)
            for n, fillers in enumerate((10, 2, 4, 2)):
                for _ in range(fillers):
                    nc.tensor.matmul(bank[QF][:, 0:P], ident[:, :], ident[:, :], start=True, stop=True)
                transposes(Block(0, 0, 0), n, T1_FIRST[n], s_xn1, s_t1)
            projection(Block(0, 0, 0), 0, QF, half=0)

            def step(prev, now, nxt):
                projection(now, 0, QF, half=1 if prev is None else None)
                projection(now, 0, QI)
                projection(now, 0, QG)
                projection(now, 1, QF)
                if is_block(prev, 0):
                    norm2_transposes(prev, 0)
                    norm2_transposes(prev, 1)
                projection(now, 1, QI)
                projection(now, 1, QG)
                if is_block(prev, 0):
                    norm2_transposes(prev, 2)
                    norm2_transposes(prev, 3)
                for q in range(3):
                    projection(now, 2, q)
                if prev is not None:
                    for n in range(NT):
                        expert_first(prev, n)
                projection(now, 3, QF)
                projection(now, 3, QI)
                projection(now, 3, QG)
                if prev is not None:
                    lora_transposes(prev)
                    expert_second(prev)
                if prev is None:
                    first_attention_out(now)
                    return
                rms_sums(now)
                for n in range(NT):
                    attention_out(now, n)
                    if nxt is None and n > 1:
                        norm2_transposes(now, n - 2)

            flow(pe, step)
            expert_first(LAST, 0)
            norm2_transposes(LAST, 2)
            expert_first(LAST, 1)
            norm2_transposes(LAST, 3)
            expert_first(LAST, 2)
            expert_first(LAST, 3)
            dst = [bank_e2(0), bank_e2(1), bank[0], bank[1]]
            pe.wait_ge(s_x1w, NT * LAST.j + 3)
            w_half(dst[0], 0, True)
            w_half(dst[1], 1, True)
            lora_transposes(LAST)
            w_half(dst[2], 2, True)
            pe.wait_ge(s_hwlo, NBLK)
            for n in range(3):
                w_then_lora(dst[n], n)
            w_half(dst[3], 3, True)
            w_then_lora(dst[3], 3)


def kernel(L0_attn_hidden_states, L0_attn_Wi, L0_attn_Wf, L0_attn_Wg, L0_attn_Wo, L0_attn_g_norm_weight,
           L0_ffn_W, L0_ffn_gate_w, L0_ffn_A, L0_ffn_B):
    import numpy as np
    import concourse.bacc as bacc
    from concourse.bass_utils import run_bass_kernel_spmd

    P = 128
    x = np.ascontiguousarray(L0_attn_hidden_states)
    D = x.shape[-1]
    NK = D // P
    E, R, _ = L0_ffn_A.shape
    wproj = np.stack([np.asarray(w).reshape(NK, P, NK, P) for w in (L0_attn_Wf, L0_attn_Wi, L0_attn_Wg)])
    wproj = wproj.transpose(3, 2, 0, 1, 4).reshape(NK, P, 3 * NK * P)
    wo = np.asarray(L0_attn_Wo).reshape(NK, P, D).transpose(1, 0, 2)
    wffn = np.concatenate([np.asarray(L0_ffn_W).T, np.asarray(L0_ffn_A).reshape(E * R, D).T, np.asarray(L0_ffn_gate_w).T], axis=1)
    wffn = wffn.reshape(NK, P, -1).transpose(1, 0, 2)
    wb = np.asarray(L0_ffn_B).transpose(0, 2, 1).reshape(E * R, D)
    gn = np.asarray(L0_attn_g_norm_weight).reshape(NK, P).T
    arrays = {"x": x, "xT": x.transpose(0, 2, 1), "gn": gn, "wproj": wproj, "wo": wo, "wffn": wffn, "wb": wb}
    arrays = {f"in_{name}": np.ascontiguousarray(a) for name, a in arrays.items()}

    nc = bacc.Bacc("TRN2", target_bir_lowering=False, num_devices=1)
    ins = [nc.dram_tensor(name, a.shape, mybir.dt.from_np(a.dtype), kind="ExternalInput").ap() for name, a in arrays.items()]
    out = nc.dram_tensor("out", x.shape, mybir.dt.from_np(x.dtype), kind="ExternalOutput").ap()
    hgrn_lora_moe(nc, *ins, out)
    return run_bass_kernel_spmd(nc, [arrays], core_ids=[0]).results[0]["out"]
```
